# Optimizing a Trainium2 kernel written in Bass

```python
import numpy as np
import jax
import jax.numpy as jnp

def _softmax(x, axis=-1):
    return jax.nn.softmax(x, axis=axis)

def _gelu(x):
    return jax.nn.gelu(x, approximate=True)

def _silu(x):
    return jax.nn.silu(x)

def _sigmoid(x):
    return jax.nn.sigmoid(x)

def _layernorm(x, axis=-1, eps=1e-05):
    m = jnp.mean(x, axis=axis, keepdims=True)
    v = jnp.var(x, axis=axis, keepdims=True)
    return (x - m) / jnp.sqrt(v + eps)

def _scatter_add(tgt, idx, src, axis=0):
    return tgt.at[idx].add(src)

def _segment_sum(src, seg, n):
    return jax.ops.segment_sum(src, seg, n)
kernel_name = 'mk_rec_standalone_d1_rec_r8_314484'

def setup_inputs(seed: int=0):
    np.random.seed(seed)
    _w = jnp.asarray

    def _rec_inputs():
        import jax
        import jax.numpy as jnp
        _rk = jax.random.key(seed)
        r_white_indices = jnp.stack([jax.random.randint(jax.random.fold_in(jax.random.fold_in(_rk, 1), 0), (2048,), 0, 4476, jnp.int32), jax.random.randint(jax.random.fold_in(jax.random.fold_in(_rk, 1), 1), (2048,), 0, 4476, jnp.int32), jax.random.randint(jax.random.fold_in(jax.random.fold_in(_rk, 1), 2), (2048,), 0, 4476, jnp.int32), jax.random.randint(jax.random.fold_in(jax.random.fold_in(_rk, 1), 3), (2048,), 0, 4476, jnp.int32), jax.random.randint(jax.random.fold_in(jax.random.fold_in(_rk, 1), 4), (2048,), 0, 4476, jnp.int32), jax.random.randint(jax.random.fold_in(jax.random.fold_in(_rk, 1), 5), (2048,), 0, 4476, jnp.int32), jax.random.randint(jax.random.fold_in(jax.random.fold_in(_rk, 1), 6), (2048,), 0, 4476, jnp.int32), jax.random.randint(jax.random.fold_in(jax.random.fold_in(_rk, 1), 7), (2048,), 0, 4476, jnp.int32), jax.random.randint(jax.random.fold_in(jax.random.fold_in(_rk, 1), 8), (2048,), 0, 4476, jnp.int32), jax.random.randint(jax.random.fold_in(jax.random.fold_in(_rk, 1), 9), (2048,), 0, 4476, jnp.int32), jax.random.randint(jax.random.fold_in(jax.random.fold_in(_rk, 1), 10), (2048,), 0, 4476, jnp.int32), jax.random.randint(jax.random.fold_in(jax.random.fold_in(_rk, 1), 11), (2048,), 0, 4476, jnp.int32), jax.random.randint(jax.random.fold_in(jax.random.fold_in(_rk, 1), 12), (2048,), 0, 4476, jnp.int32), jax.random.randint(jax.random.fold_in(jax.random.fold_in(_rk, 1), 13), (2048,), 0, 4476, jnp.int32), jax.random.randint(jax.random.fold_in(jax.random.fold_in(_rk, 1), 14), (2048,), 0, 4476, jnp.int32), jax.random.randint(jax.random.fold_in(jax.random.fold_in(_rk, 1), 15), (2048,), 0, 4476, jnp.int32), jax.random.randint(jax.random.fold_in(jax.random.fold_in(_rk, 1), 16), (2048,), 0, 4476, jnp.int32), jax.random.randint(jax.random.fold_in(jax.random.fold_in(_rk, 1), 17), (2048,), 0, 4476, jnp.int32), jax.random.randint(jax.random.fold_in(jax.random.fold_in(_rk, 1), 18), (2048,), 0, 4476, jnp.int32), jax.random.randint(jax.random.fold_in(jax.random.fold_in(_rk, 1), 19), (2048,), 1, 4476, jnp.int32), jax.random.randint(jax.random.fold_in(jax.random.fold_in(_rk, 1), 20), (2048,), 0, 4476, jnp.int32), jax.random.randint(jax.random.fold_in(jax.random.fold_in(_rk, 1), 21), (2048,), 0, 4476, jnp.int32), jax.random.randint(jax.random.fold_in(jax.random.fold_in(_rk, 1), 22), (2048,), 0, 4476, jnp.int32), jax.random.randint(jax.random.fold_in(jax.random.fold_in(_rk, 1), 23), (2048,), 0, 4476, jnp.int32), jax.random.randint(jax.random.fold_in(jax.random.fold_in(_rk, 1), 24), (2048,), 0, 4476, jnp.int32), jax.random.randint(jax.random.fold_in(jax.random.fold_in(_rk, 1), 25), (2048,), 0, 4476, jnp.int32), jax.random.randint(jax.random.fold_in(jax.random.fold_in(_rk, 1), 26), (2048,), 0, 4476, jnp.int32), jax.random.randint(jax.random.fold_in(jax.random.fold_in(_rk, 1), 27), (2048,), 0, 4476, jnp.int32), jax.random.randint(jax.random.fold_in(jax.random.fold_in(_rk, 1), 28), (2048,), 0, 4476, jnp.int32), jax.random.randint(jax.random.fold_in(jax.random.fold_in(_rk, 1), 29), (2048,), 0, 4476, jnp.int32)], axis=1)
        r_black_indices = jnp.stack([jax.random.randint(jax.random.fold_in(jax.random.fold_in(_rk, 2), 0), (2048,), 0, 4476, jnp.int32), jax.random.randint(jax.random.fold_in(jax.random.fold_in(_rk, 2), 1), (2048,), 0, 4476, jnp.int32), jax.random.randint(jax.random.fold_in(jax.random.fold_in(_rk, 2), 2), (2048,), 0, 4476, jnp.int32), jax.random.randint(jax.random.fold_in(jax.random.fold_in(_rk, 2), 3), (2048,), 0, 4476, jnp.int32), jax.random.randint(jax.random.fold_in(jax.random.fold_in(_rk, 2), 4), (2048,), 0, 4476, jnp.int32), jax.random.randint(jax.random.fold_in(jax.random.fold_in(_rk, 2), 5), (2048,), 0, 4476, jnp.int32), jax.random.randint(jax.random.fold_in(jax.random.fold_in(_rk, 2), 6), (2048,), 0, 4475, jnp.int32), jax.random.randint(jax.random.fold_in(jax.random.fold_in(_rk, 2), 7), (2048,), 0, 4476, jnp.int32), jax.random.randint(jax.random.fold_in(jax.random.fold_in(_rk, 2), 8), (2048,), 0, 4476, jnp.int32), jax.random.randint(jax.random.fold_in(jax.random.fold_in(_rk, 2), 9), (2048,), 0, 4476, jnp.int32), jax.random.randint(jax.random.fold_in(jax.random.fold_in(_rk, 2), 10), (2048,), 0, 4476, jnp.int32), jax.random.randint(jax.random.fold_in(jax.random.fold_in(_rk, 2), 11), (2048,), 0, 4476, jnp.int32), jax.random.randint(jax.random.fold_in(jax.random.fold_in(_rk, 2), 12), (2048,), 0, 4476, jnp.int32), jax.random.randint(jax.random.fold_in(jax.random.fold_in(_rk, 2), 13), (2048,), 0, 4476, jnp.int32), jax.random.randint(jax.random.fold_in(jax.random.fold_in(_rk, 2), 14), (2048,), 0, 4476, jnp.int32), jax.random.randint(jax.random.fold_in(jax.random.fold_in(_rk, 2), 15), (2048,), 0, 4476, jnp.int32), jax.random.randint(jax.random.fold_in(jax.random.fold_in(_rk, 2), 16), (2048,), 0, 4476, jnp.int32), jax.random.randint(jax.random.fold_in(jax.random.fold_in(_rk, 2), 17), (2048,), 0, 4476, jnp.int32), jax.random.randint(jax.random.fold_in(jax.random.fold_in(_rk, 2), 18), (2048,), 0, 4476, jnp.int32), jax.random.randint(jax.random.fold_in(jax.random.fold_in(_rk, 2), 19), (2048,), 0, 4476, jnp.int32), jax.random.randint(jax.random.fold_in(jax.random.fold_in(_rk, 2), 20), (2048,), 0, 4476, jnp.int32), jax.random.randint(jax.random.fold_in(jax.random.fold_in(_rk, 2), 21), (2048,), 0, 4476, jnp.int32), jax.random.randint(jax.random.fold_in(jax.random.fold_in(_rk, 2), 22), (2048,), 0, 4476, jnp.int32), jax.random.randint(jax.random.fold_in(jax.random.fold_in(_rk, 2), 23), (2048,), 0, 4476, jnp.int32), jax.random.randint(jax.random.fold_in(jax.random.fold_in(_rk, 2), 24), (2048,), 0, 4476, jnp.int32), jax.random.randint(jax.random.fold_in(jax.random.fold_in(_rk, 2), 25), (2048,), 0, 4476, jnp.int32), jax.random.randint(jax.random.fold_in(jax.random.fold_in(_rk, 2), 26), (2048,), 0, 4476, jnp.int32), jax.random.randint(jax.random.fold_in(jax.random.fold_in(_rk, 2), 27), (2048,), 0, 4476, jnp.int32), jax.random.randint(jax.random.fold_in(jax.random.fold_in(_rk, 2), 28), (2048,), 0, 4476, jnp.int32), jax.random.randint(jax.random.fold_in(jax.random.fold_in(_rk, 2), 29), (2048,), 0, 4476, jnp.int32)], axis=1)
        return (r_white_indices, r_black_indices)
    r_white_indices, r_black_indices = _rec_inputs()

    def _L0_rec_setup():
        import jax, jax.numpy as jnp
        import numpy as np
        FEATURE_COUNT = 4476
        NUM_ACTIVE = 30
        BATCH = 2048
        HIDDEN = 512

        def _one_hot_features(indices):
            B = indices.shape[0]
            feats = jnp.zeros((B, FEATURE_COUNT), jnp.float32)
            batch_idx = jnp.broadcast_to(jnp.arange(B)[:, None], indices.shape)
            return feats.at[batch_idx, indices].set(1.0)
        key = jax.random.key(seed)
        ks = jax.random.split(key, 8)
        return {'white_indices': jax.random.randint(ks[0], (BATCH, NUM_ACTIVE), 0, FEATURE_COUNT), 'black_indices': jax.random.randint(ks[1], (BATCH, NUM_ACTIVE), 0, FEATURE_COUNT), 'ft_w': jax.random.normal(ks[2], (HIDDEN, FEATURE_COUNT), jnp.float32) * 0.1, 'w1': jax.random.normal(ks[3], (HIDDEN, 2 * HIDDEN), jnp.float32) * 0.1, 'b1': jnp.zeros((HIDDEN,), jnp.float32), 'w2': jax.random.normal(ks[4], (HIDDEN // 2, HIDDEN), jnp.float32) * 0.1, 'b2': jnp.zeros((HIDDEN // 2,), jnp.float32), 'w3': jax.random.normal(ks[5], (HIDDEN // 4, HIDDEN // 2), jnp.float32) * 0.1, 'b3': jnp.zeros((HIDDEN // 4,), jnp.float32), 'wo': jax.random.normal(ks[6], (1, HIDDEN // 4), jnp.float32) * 0.1, 'bo': jnp.zeros((1,), jnp.float32)}
    _L0_rec_all = _L0_rec_setup()
    _L0_rec_in = {k: v for k, v in _L0_rec_all.items() if k in ('ft_w', 'w1', 'b1', 'w2', 'b2', 'w3', 'b3', 'wo', 'bo')}
    del _L0_rec_all
    return {'r_white_indices': r_white_indices, 'r_black_indices': r_black_indices, 'L0_rec_ft_w': _L0_rec_in['ft_w'], 'L0_rec_w1': _L0_rec_in['w1'], 'L0_rec_b1': _L0_rec_in['b1'], 'L0_rec_w2': _L0_rec_in['w2'], 'L0_rec_b2': _L0_rec_in['b2'], 'L0_rec_w3': _L0_rec_in['w3'], 'L0_rec_b3': _L0_rec_in['b3'], 'L0_rec_wo': _L0_rec_in['wo'], 'L0_rec_bo': _L0_rec_in['bo']}

def reference(r_white_indices, r_black_indices, L0_rec_ft_w, L0_rec_w1, L0_rec_b1, L0_rec_w2, L0_rec_b2, L0_rec_w3, L0_rec_b3, L0_rec_wo, L0_rec_bo):
    import jax
    import jax.numpy as jnp

    def _L0_rec_ref(white_indices, black_indices, ft_w, w1, b1, w2, b2, w3, b3, wo, bo):
        import jax, jax.numpy as jnp
        import numpy as np
        FEATURE_COUNT = 4476
        NUM_ACTIVE = 30
        BATCH = 2048
        HIDDEN = 512

        def _one_hot_features(indices):
            B = indices.shape[0]
            feats = jnp.zeros((B, FEATURE_COUNT), jnp.float32)
            batch_idx = jnp.broadcast_to(jnp.arange(B)[:, None], indices.shape)
            return feats.at[batch_idx, indices].set(1.0)

        def transform(idx):
            feats = _one_hot_features(idx)
            return jnp.clip(feats @ ft_w.T, -1.0, 1.0)
        w = transform(white_indices)
        b = transform(black_indices)
        h = jnp.concatenate([w, b], axis=1)
        h = jax.nn.relu(h @ w1.T + b1)
        h = jax.nn.relu(h @ w2.T + b2)
        h = jax.nn.relu(h @ w3.T + b3)
        out = h @ wo.T + bo
        return out.squeeze(-1)
    y = _L0_rec_ref(r_white_indices, r_black_indices, L0_rec_ft_w, L0_rec_w1, L0_rec_b1, L0_rec_w2, L0_rec_b2, L0_rec_w3, L0_rec_b3, L0_rec_wo, L0_rec_bo)
    return y

_drawn_inputs = setup_inputs


def setup_inputs(seed=0):
    import zlib

    import numpy as np

    out = dict(_drawn_inputs(seed))
    spreads = {'L0_rec_b1': (0.0, 0.1), 'L0_rec_b2': (0.0, 0.1), 'L0_rec_b3': (0.0, 0.1)}
    factors = {}
    for name, (base, spread) in spreads.items():
        noise = np.random.default_rng([zlib.crc32(name.encode()), seed]).standard_normal(out[name].shape)
        drawn = base * np.exp(spread * noise) if base else spread * noise
        out[name] = jnp.asarray(drawn.astype(out[name].dtype))
    for name, factor in factors.items():
        out[name] = (out[name] * factor).astype(out[name].dtype)
    return out
```

```python
import concourse.bass as bass
from concourse import mybir
from contextlib import ExitStack

SIDES = 2
ACTIVE = 30
FEATURES = 4476
HIDDEN = 512
BATCH = 2048
TILE = 128
HIGHS = -(-FEATURES // TILE)
PADDED = HIGHS * TILE
CHUNK = 512
PAIRS = BATCH // CHUNK
ROWS = 4
QUADS = CHUNK // ROWS
PAIRS_OF_INDICES = ROWS * ACTIVE
GROUP = 4
GROUPS = QUADS // GROUP
COUNTS = HIGHS * ROWS
COUNT_STRIDE = 256
UNIT_TILES = HIDDEN // TILE
SECTIONS = 5
SECTION = HIGHS // SECTIONS
SECTION_COLUMNS = SECTION * TILE
RING = 4
H1 = 512
H2 = 256
H3 = 128
MAX_FLOAT_EXPONENT_PAIR = 254
SCALED_EXPONENT = 14


def nnue_kernel(nc, indices, tables, ft_w, w1, w2, w3, biases, bo, out):
    F32, F16, I32 = mybir.dt.float32, mybir.dt.float16, mybir.dt.int32
    ALU, ACT, AX = mybir.AluOpType, mybir.ActivationFunctionType, mybir.AxisListType

    ctx = ExitStack()
    with ctx:
        def sb(name, shape, dt):
            return ctx.enter_context(nc.sbuf_tensor(name, shape, dt))

        def pb(name, shape, dt):
            return ctx.enter_context(nc.psum_tensor(name, shape, dt))

        def sem(name):
            return ctx.enter_context(nc.semaphore(name))

        weights = sb("weights", [TILE, 2, HIGHS, HIDDEN], F16)
        multihot = [sb(f"multihot{i}", [TILE, HIGHS, CHUNK], F16) for i in range(SIDES)]
        mlp_region = sb("mlp_region", [TILE, 8 * H1 + 4 * H2 + 2 * H3], F32)
        hidden0 = sb("hidden0", [TILE, SIDES * UNIT_TILES, CHUNK], F32)
        hidden1 = sb("hidden1", [TILE, H1 // TILE, CHUNK], F32)
        small_region = sb("small_region", [TILE, 2 * 2 * SECTION_COLUMNS], F16)
        high_hot = sb("high_hot", [PAIRS_OF_INDICES, RING, GROUP, COUNTS], F16)
        low_hot = sb("low_hot", [PAIRS_OF_INDICES, RING, GROUP, TILE], F16)
        index = sb("index", [PAIRS_OF_INDICES, PAIRS * SIDES, QUADS], I32)
        high = sb("high", [PAIRS_OF_INDICES, SIDES, QUADS], F32)
        low = sb("low", [PAIRS_OF_INDICES, SIDES, QUADS], F32)
        table = sb("table", [TILE, COUNTS + TILE + TILE], F16)
        high_codes = table[0:PAIRS_OF_INDICES, 0:COUNTS]
        low_codes = table[0:PAIRS_OF_INDICES, COUNTS:COUNTS + TILE]
        identity = table[:, COUNTS + TILE:COUNTS + 2 * TILE]
        largest = sb("largest", [TILE, UNIT_TILES], F32)
        power = sb("power", [TILE, UNIT_TILES], I32)
        unscale = sb("unscale", [TILE, UNIT_TILES], F32)
        scale = sb("scale", [TILE, UNIT_TILES], F32)
        bias = sb("bias", [TILE, 8], F32)
        bias_out = sb("bias_out", [1, 1], F32)

        stage_words = PADDED
        stages = [multihot[1][:, :, :].rearrange("p k n -> p (k n)")
                  [:, 2 * stage_words * i:2 * stage_words * (i + 1)].bitcast(F32) for i in range(2)]
        stages += [mlp_region[:, 0:stage_words]] * 2
        w1_sb = mlp_region[:, 0:8 * H1].rearrange("p (k n) -> p k n", n=H1)
        w2_sb = mlp_region[:, 8 * H1:8 * H1 + 4 * H2].rearrange("p (k n) -> p k n", n=H2)
        w3_sb = mlp_region[:, 8 * H1 + 4 * H2:].rearrange("p (k n) -> p k n", n=H3)
        split = small_region[:, :].rearrange("p (s h n) -> p s h n", s=2, h=2)
        hidden2 = small_region[:, 0:2 * 2 * CHUNK].bitcast(F32).rearrange("p (k n) -> p k n", n=CHUNK)
        hidden3 = small_region[:, 4 * CHUNK:6 * CHUNK].bitcast(F32)
        scores = hidden2[0:1, 0, :]

        transform = pb("transform", [TILE, 2, CHUNK], F32)
        counts = pb("counts", [TILE, 2, GROUP, COUNT_STRIDE], F32)
        layer = pb("layer", [TILE, 2, CHUNK], F32)
        turned = [layer[:, i, :].bitcast(F16)[:, 0:SECTION_COLUMNS] for i in range(2)]

        index_loaded = sem("index_loaded")
        table_loaded = sem("table_loaded")
        stage_loaded = [sem(f"stage{m}_loaded") for m in range(UNIT_TILES)]
        mlp_loaded = sem("mlp_loaded")
        bias_loaded = sem("bias_loaded")
        pad_cleared = sem("pad_cleared")
        chunk_split = sem("chunk_split")
        onehots_ready = sem("onehots_ready")
        counted = sem("counted")
        multihot_ready = sem("multihot_ready")
        scale_steps = sem("scale_steps")
        high_split = sem("high_split")
        low_split = sem("low_split")
        high_turned = sem("high_turned")
        low_turned = sem("low_turned")
        high_placed = sem("high_placed")
        low_placed = sem("low_placed")
        transform_done = sem("transform_done")
        transform_read = sem("transform_read")
        hidden0_ready = sem("hidden0_ready")
        layer_done = sem("layer_done")
        layer_read = sem("layer_read")
        stored = sem("stored")

        LAYER_BANKS = H1 // TILE + H2 // TILE + H3 // TILE + 1
        block = ctx.enter_context(nc.Block())

        @block.sync
        def _(sp):
            sp.dma_start(index[:, :, :], indices).then_inc(index_loaded, 16)
            for m in range(3):
                sp.dma_start(stages[m][:, 0:FEATURES], ft_w[m * TILE:(m + 1) * TILE, :])\
                    .then_inc(stage_loaded[m], 16)
            sp.wait_ge(high_split, 3 * SECTIONS)
            sp.wait_ge(low_split, 3 * SECTIONS)
            sp.dma_start(stages[3][:, 0:FEATURES], ft_w[3 * TILE:4 * TILE, :])\
                .then_inc(stage_loaded[3], 16)
            sp.wait_ge(high_split, 4 * SECTIONS)
            sp.wait_ge(low_split, 4 * SECTIONS)
            sp.dma_start(w1_sb, w1).then_inc(mlp_loaded, 16)
            sp.dma_start(w2_sb, w2).then_inc(mlp_loaded, 16)
            sp.dma_start(w3_sb, w3).then_inc(mlp_loaded, 16)

            with sp.Fori(0, PAIRS) as pair:
                sp.wait_ge(layer_read, LAYER_BANKS * pair + LAYER_BANKS)
                sp.dma_start(out[0:1, bass.ds(pair * CHUNK, CHUNK)], scores).then_inc(stored, 16)
            sp.wait_ge(stored, 16 * PAIRS)

        @block.gpsimd
        def _(pool):
            for stage in stages[0:3]:
                nc.gpsimd.memset(stage[:, FEATURES:PADDED], 0.0).then_inc(pad_cleared, 1)

        @block.vector
        def _(dve):
            def split_indices(chunk, side):
                slot = side
                steps = 3 * chunk
                high_int = low[:, slot, :].bitcast(I32)
                nc.vector.tensor_scalar(high_int, index[:, bass.ds(chunk, 1), :], 7, None,
                                        ALU.arith_shift_right).then_inc(chunk_split, 1)
                dve.wait_ge(chunk_split, steps + 1)
                nc.vector.tensor_copy(high[:, slot, :], high_int).then_inc(chunk_split, 1)
                dve.wait_ge(chunk_split, steps + 2)
                nc.vector.scalar_tensor_tensor(out=low[:, slot, :], in0=high[:, slot, :],
                                               scalar=-float(TILE), in1=index[:, bass.ds(chunk, 1), :],
                                               op0=ALU.mult, op1=ALU.add).then_inc(chunk_split, 1)

            def compare(group, slot, first_quad, side, ring_full):
                if ring_full:
                    dve.wait_ge(counted, group - (RING - 1))
                for q in range(GROUP):
                    quad = first_quad + q
                    nc.vector.tensor_scalar(high_hot[:, slot, q, :], high_codes,
                                            high[:, side, bass.ds(quad, 1)], None, ALU.is_equal)
                    last = nc.vector.tensor_scalar(low_hot[:, slot, q, :], low_codes,
                                                   low[:, side, bass.ds(quad, 1)], None, ALU.is_equal)
                last.then_inc(onehots_ready, 1)

            def weight_scale(m):
                dve.wait_ge(stage_loaded[m], 16)
                dve.wait_ge(pad_cleared, min(m, 2) + 1)
                column = slice(m, m + 1)
                nc.vector.tensor_reduce(largest[:, column], stages[m][:, :], AX.X, ALU.max,
                                        apply_absolute_value=True).then_inc(scale_steps, 1)
                dve.wait_ge(scale_steps, 4 * m + 1)
                nc.vector.tensor_scalar(power[:, column], largest[:, column].bitcast(I32), 0xFF << 23, None,
                                        ALU.bitwise_and).then_inc(scale_steps, 1)
                dve.wait_ge(scale_steps, 4 * m + 2)
                nc.vector.tensor_scalar(unscale[:, column].bitcast(I32), power[:, column],
                                        float((SCALED_EXPONENT + 1) << 23), float(SCALED_EXPONENT << 23),
                                        ALU.max, ALU.subtract).then_inc(scale_steps, 1)
                dve.wait_ge(scale_steps, 4 * m + 3)
                nc.vector.tensor_scalar(scale[:, column].bitcast(I32), unscale[:, column].bitcast(I32),
                                        -1.0, float(MAX_FLOAT_EXPONENT_PAIR << 23),
                                        ALU.mult, ALU.add).then_inc(scale_steps, 1)
                dve.wait_ge(scale_steps, 4 * m + 4)

            def split_low(m, s):
                n = m * SECTIONS + s
                dve.wait_ge(high_split, n + 1)
                if n >= 2:
                    dve.wait_ge(low_turned, n - 1)
                columns = slice(s * SECTION_COLUMNS, (s + 1) * SECTION_COLUMNS)
                nc.vector.scalar_tensor_tensor(out=split[:, n % 2, 1, :], in0=stages[m][:, columns],
                                               scalar=scale[:, m:m + 1], in1=split[:, n % 2, 0, :],
                                               op0=ALU.mult, op1=ALU.subtract).then_inc(low_split, 1)

            def place_low(m, s):
                n = m * SECTIONS + s
                dve.wait_ge(low_turned, n + 1)
                nc.vector.tensor_copy(weights[:, 1, s * SECTION:(s + 1) * SECTION, m * TILE:(m + 1) * TILE],
                                      turned[1].rearrange("p (k n) -> p k n", n=TILE))\
                    .then_inc(low_placed, 1)

            def clip(unit_tile, bank, row, m):
                dve.wait_ge(transform_done, unit_tile + 1)
                nc.vector.tensor_scalar(hidden0[:, row, :], transform[:, bank, :],
                                        unscale[:, bass.ds(m, 1)], 1.0, ALU.mult, ALU.min)\
                    .then_inc(transform_read, 1)
                dve.wait_ge(transform_read, unit_tile + 1)
                nc.vector.tensor_scalar(hidden0[:, row, :], hidden0[:, row, :], -1.0, None, ALU.max)\
                    .then_inc(hidden0_ready, 1)

            dve.wait_ge(index_loaded, 16)
            dve.wait_ge(table_loaded, 16)
            split_indices(0, 0)
            dve.wait_ge(chunk_split, 3)
            for g in range(GROUPS):
                compare(g, g % RING, g * GROUP, 0, g >= RING)
            weight_scale(0)
            for s in range(SECTIONS):
                split_low(0, s)
                if s:
                    place_low(0, s - 1)
            place_low(0, SECTIONS - 1)
            split_indices(1, 1)
            dve.wait_ge(chunk_split, 6)
            for m in range(UNIT_TILES):
                if m + 1 < UNIT_TILES:
                    weight_scale(m + 1)
                    split_low(m + 1, 0)
                for s in range(SECTIONS):
                    for g in first_chunk_groups(m, s):
                        compare(GROUPS + g, g % RING, g * GROUP, 1, True)
                    if m + 1 < UNIT_TILES:
                        if s + 1 < SECTIONS:
                            split_low(m + 1, s + 1)
                        place_low(m + 1, s)
                clip(m, m % 2, m, m)

            def products_of(chunk, side, groups_a_tile, next_chunk_groups):
                with dve.Fori(0, UNIT_TILES // 2) as half:
                    dve.wait_ge(chunk_split, 3 * chunk + 6)
                    for parity in range(2):
                        m = 2 * half + parity
                        for j in range(groups_a_tile):
                            g = groups_a_tile * m + j
                            step = (groups_a_tile * parity + j) % RING
                            compare(next_chunk_groups + g, step, g * GROUP, 1 - side, True)
                        clip(UNIT_TILES * chunk + m, parity, UNIT_TILES * side + m, m)

            with dve.Fori(0, PAIRS - 1) as pair:
                black = 2 * pair + 1
                split_indices(black + 1, 0)
                products_of(black, 1, B_GROUPS, GROUPS * (black + 1))
                for g in range(UNIT_TILES * B_GROUPS, GROUPS):
                    compare(GROUPS * (black + 1) + g, g % RING, g * GROUP, 0, True)
                split_indices(black + 2, 1)
                products_of(black + 1, 0, A_GROUPS, GROUPS * (black + 2))
            for m in range(UNIT_TILES):
                clip(UNIT_TILES * (2 * PAIRS - 1) + m, m % 2, UNIT_TILES + m, m)

        @block.scalar
        def _(act):
            act.dma_start(table[:, :], tables).then_inc(table_loaded, 16)
            act.dma_start(bias[:, :], biases).then_inc(bias_loaded, 16)
            act.dma_start(bias_out[:, :], bo).then_inc(bias_loaded, 16)

            def place_multihot(group, bank, quad_columns, side):
                act.wait_ge(counted, group + 1)
                nc.scalar.activation(
                    multihot[side][:, :, quad_columns].rearrange("p h (q b) -> p h q b", b=ROWS),
                    counts[:, bank, :, 0:COUNTS].rearrange("p q (h b) -> p h q b", b=ROWS),
                    ACT.Sign).then_inc(multihot_ready, 1)

            def split_high(m, s):
                n = m * SECTIONS + s
                if s == 0:
                    act.wait_ge(scale_steps, 4 * m + 4)
                if n >= 2:
                    act.wait_ge(low_split, n - 1)
                    act.wait_ge(high_turned, n - 1)
                columns = slice(s * SECTION_COLUMNS, (s + 1) * SECTION_COLUMNS)
                nc.scalar.activation(split[:, n % 2, 0, :], stages[m][:, columns], ACT.Copy,
                                     scale=scale[:, m:m + 1]).then_inc(high_split, 1)

            def place_high(m, s):
                n = m * SECTIONS + s
                act.wait_ge(high_turned, n + 1)
                nc.scalar.activation(weights[:, 0, s * SECTION:(s + 1) * SECTION, m * TILE:(m + 1) * TILE],
                                     turned[0].rearrange("p (k n) -> p k n", n=TILE), ACT.Copy)\
                    .then_inc(high_placed, 1)

            def columns_of(g):
                return slice(g * GROUP * ROWS, (g + 1) * GROUP * ROWS)

            def columns_at(g):
                return bass.ds(g * (GROUP * ROWS), GROUP * ROWS)

            for g in range(GROUPS):
                place_multihot(g, g % 2, columns_of(g), 0)
            for s in range(SECTIONS):
                split_high(0, s)
                if s:
                    place_high(0, s - 1)
            place_high(0, SECTIONS - 1)
            for m in range(UNIT_TILES):
                if m + 1 < UNIT_TILES:
                    split_high(m + 1, 0)
                for s in range(SECTIONS):
                    groups = first_chunk_groups(m, s)
                    if groups and groups[0] == 0:
                        act.wait_ge(low_split, 2 * SECTIONS)
                        act.wait_ge(high_split, 2 * SECTIONS)
                    for g in groups:
                        place_multihot(GROUPS + g, g % 2, columns_of(g), 1)
                    if m + 1 < UNIT_TILES:
                        if s + 1 < SECTIONS:
                            split_high(m + 1, s + 1)
                        place_high(m + 1, s)

            def place_groups(first_group, side, groups_a_tile):
                with act.Fori(0, UNIT_TILES // 2) as half:
                    for j in range(2 * groups_a_tile):
                        g = 2 * groups_a_tile * half + j
                        place_multihot(first_group + g, j % 2, columns_at(g), side)

            def relu_layer(pair, bank_number, to, bias_column):
                act.wait_ge(layer_done, LAYER_BANKS * pair + bank_number + 1)
                nc.scalar.activation(to, layer[:, bank_number % 2, :], ACT.Relu,
                                     bias=bias[:, bias_column:bias_column + 1]).then_inc(layer_read, 1)

            def later_layers(pair, between):
                for t in range(H1 // TILE):
                    relu_layer(pair, t, hidden1[:, t, :], t)
                between(0)
                for t in range(H2 // TILE):
                    relu_layer(pair, 4 + t, hidden2[:, t, :], 4 + t)
                between(1)
                relu_layer(pair, 6, hidden3, 6)
                between(2)
                act.wait_ge(layer_done, LAYER_BANKS * pair + 8)
                nc.scalar.activation(scores, layer[0:1, 1, :], ACT.Identity, bias=bias_out[:, :])\
                    .then_inc(layer_read, 1)

            act.wait_ge(bias_loaded, 32)
            with act.Fori(0, PAIRS - 1) as pair:
                black = 2 * pair + 1
                place_groups(GROUPS * (black + 1), 0, B_GROUPS)

                def between(gap):
                    for g in filler_groups(gap):
                        place_multihot(GROUPS * (black + 1) + g, g % 2, columns_of(g), 0)

                later_layers(pair, between)
                place_groups(GROUPS * (black + 2), 1, A_GROUPS)
                act.wait_ge(stored, 16 * pair + 16)
            later_layers(PAIRS - 1, lambda gap: None)

        @block.tensor
        def _(pe):
            def count(group, slot, bank, first=False):
                pe.wait_ge(onehots_ready, group + 1)
                if not first:
                    pe.wait_ge(multihot_ready, group - 1)
                for q in range(GROUP):
                    last = nc.tensor.matmul(counts[:, bank, q, 0:COUNTS], low_hot[:, slot, q, :],
                                            high_hot[:, slot, q, :], start=True, stop=True)
                last.then_inc(counted, 1)

            def turn(m, s):
                n = m * SECTIONS + s
                for part, was_split, was_placed, was_turned in (
                        (0, high_split, high_placed, high_turned), (1, low_split, low_placed, low_turned)):
                    pe.wait_ge(was_split, n + 1)
                    if n:
                        pe.wait_ge(was_placed, n)
                    for k in range(SECTION):
                        last = nc.tensor.transpose(turned[part][:, k * TILE:(k + 1) * TILE],
                                                   split[:, n % 2, part, k * TILE:(k + 1) * TILE], identity)
                    last.then_inc(was_turned, 1)

            def multiply(side, units, bank, s):
                for k in range(s * SECTION, (s + 1) * SECTION):
                    for part in range(2):
                        last = nc.tensor.matmul(transform[:, bank, :], weights[:, part, k, units],
                                                multihot[side][:, k, :], start=(k == 0 and part == 0),
                                                stop=(k == HIGHS - 1 and part == 1))
                return last

            pe.wait_ge(table_loaded, 16)
            for g in range(GROUPS):
                count(g, g % RING, g % 2, first=g < 2)
            for s in range(SECTIONS):
                turn(0, s)
            for m in range(UNIT_TILES):
                if m >= 2:
                    pe.wait_ge(transform_read, m - 1)
                if m == 0:
                    pe.wait_ge(multihot_ready, GROUPS)
                for s in range(SECTIONS):
                    pe.wait_ge(high_placed, m * SECTIONS + s + 1)
                    pe.wait_ge(low_placed, m * SECTIONS + s + 1)
                    last = multiply(0, slice(m * TILE, (m + 1) * TILE), m % 2, s)
                    if s == SECTIONS - 1:
                        last.then_inc(transform_done, 1)
                    for g in first_chunk_groups(m, s):
                        count(GROUPS + g, g % RING, g % 2)
                    if m + 1 < UNIT_TILES:
                        turn(m + 1, s)

            def multiply_chunk(chunk, side, groups_a_tile, next_group):
                with pe.Fori(0, UNIT_TILES // 2) as half:
                    pe.wait_ge(multihot_ready, GROUPS * chunk + GROUPS)
                    for parity in range(2):
                        pe.wait_ge(transform_read, UNIT_TILES * chunk + 2 * half + parity - 1)
                        units = bass.ds((2 * half + parity) * TILE, TILE)
                        done = 0
                        for s in range(SECTIONS):
                            last = multiply(side, units, parity, s)
                            if s == SECTIONS - 1:
                                last.then_inc(transform_done, 1)
                            while done < groups_a_tile * (s + 1) // SECTIONS:
                                j = groups_a_tile * parity + done
                                count(next_group + 2 * groups_a_tile * half + j, j % RING, j % 2)
                                done += 1

            def later_layers(pair, between):
                banks = LAYER_BANKS * pair
                pe.wait_ge(hidden0_ready, 8 * pair + 7)
                for t in range(H1 // TILE):
                    if t >= 2:
                        pe.wait_ge(layer_read, banks + t - 1)
                    for k in range(SIDES * UNIT_TILES):
                        if t == 0 and k == SIDES * UNIT_TILES - 1:
                            pe.wait_ge(hidden0_ready, 8 * pair + 8)
                        last = nc.tensor.matmul(layer[:, t % 2, :], w1_sb[:, k, t * TILE:(t + 1) * TILE],
                                                hidden0[:, k, :], start=(k == 0),
                                                stop=(k == SIDES * UNIT_TILES - 1))
                    last.then_inc(layer_done, 1)
                between(0)
                for t in range(H2 // TILE):
                    pe.wait_ge(layer_read, banks + 4)
                    for k in range(H1 // TILE):
                        last = nc.tensor.matmul(layer[:, t % 2, :], w2_sb[:, k, t * TILE:(t + 1) * TILE],
                                                hidden1[:, k, :], start=(k == 0), stop=(k == H1 // TILE - 1))
                    last.then_inc(layer_done, 1)
                between(1)
                pe.wait_ge(layer_read, banks + 6)
                for k in range(H2 // TILE):
                    last = nc.tensor.matmul(layer[:, 0, :], w3_sb[:, k, :], hidden2[:, k, :],
                                            start=(k == 0), stop=(k == H2 // TILE - 1))
                last.then_inc(layer_done, 1)
                between(2)
                pe.wait_ge(layer_read, banks + 7)
                nc.tensor.matmul(layer[0:1, 1, :], bias[:, 7:8], hidden3, start=True, stop=True)\
                    .then_inc(layer_done, 1)

            pe.wait_ge(mlp_loaded, 48)
            pe.wait_ge(bias_loaded, 32)
            with pe.Fori(0, PAIRS - 1) as pair:
                black = 2 * pair + 1
                multiply_chunk(black, 1, B_GROUPS, GROUPS * (black + 1))

                def between(gap):
                    for g in filler_groups(gap):
                        count(GROUPS * (black + 1) + g, g % RING, g % 2)

                later_layers(pair, between)
                multiply_chunk(black + 1, 0, A_GROUPS, GROUPS * (black + 2))
                pe.wait_ge(layer_read, LAYER_BANKS * pair + LAYER_BANKS)
            pe.wait_ge(multihot_ready, GROUPS * SIDES * PAIRS)
            for m in range(UNIT_TILES):
                pe.wait_ge(transform_read, UNIT_TILES * (SIDES * PAIRS - 1) + m - 1)
                for s in range(SECTIONS):
                    last = multiply(1, slice(m * TILE, (m + 1) * TILE), m % 2, s)
                last.then_inc(transform_done, 1)
            later_layers(PAIRS - 1, lambda gap: None)


B_GROUPS = 6
A_GROUPS = GROUPS // UNIT_TILES


def filler_groups(gap):
    ends = [UNIT_TILES * B_GROUPS, 26, 29, GROUPS]
    return range(ends[gap], ends[gap + 1])


def first_chunk_groups(m, s):
    ends = [0] * SECTIONS + [2 * (i + 1) for i in range(2 * SECTIONS)] + [23, 26, 28, 30, GROUPS]
    n = m * SECTIONS + s
    return range(ends[n - 1] if n else 0, ends[n])


def kernel(**inputs):
    import numpy as np
    import concourse.bacc as bacc
    from concourse.bass_utils import run_bass_kernel_spmd

    def side(name):
        a = np.asarray(inputs[name]).reshape(PAIRS, QUADS, ROWS, ACTIVE)
        return a.transpose(2, 3, 0, 1).reshape(PAIRS_OF_INDICES, PAIRS, QUADS)

    def tiled(name):
        a = np.asarray(inputs["L0_rec_" + name]).T
        return np.ascontiguousarray(a.reshape(-1, TILE, a.shape[1]).transpose(1, 0, 2))

    def columns(name):
        return np.asarray(inputs["L0_rec_" + name]).reshape(-1, TILE).T

    table = np.zeros((TILE, COUNTS + 2 * TILE), np.float16)
    owner = np.arange(PAIRS_OF_INDICES)[:, None, None] // ACTIVE
    codes = np.where(np.arange(ROWS)[None, None, :] == owner, np.arange(HIGHS)[None, :, None], -1)
    table[0:PAIRS_OF_INDICES, 0:COUNTS] = codes.reshape(PAIRS_OF_INDICES, COUNTS)
    table[:, COUNTS:COUNTS + TILE] = np.arange(TILE)
    table[:, COUNTS + TILE:] = np.eye(TILE)

    arrays = {
        "indices": np.ascontiguousarray(np.stack([side("r_white_indices"), side("r_black_indices")], axis=2)
                                        .reshape(PAIRS_OF_INDICES, SIDES * PAIRS, QUADS)),
        "tables": table,
        "ft_w": np.ascontiguousarray(inputs["L0_rec_ft_w"]),
        "w1": tiled("w1"), "w2": tiled("w2"), "w3": tiled("w3"),
        "biases": np.ascontiguousarray(np.concatenate(
            [columns("b1"), columns("b2"), columns("b3"), columns("wo")], axis=1)),
        "bo": np.asarray(inputs["L0_rec_bo"]).reshape(1, 1),
    }
    nc = bacc.Bacc("TRN2", target_bir_lowering=False, num_devices=1)
    args = {name: nc.dram_tensor(f"{name}_dram", a.shape, mybir.dt.from_np(a.dtype), kind="ExternalInput").ap()
            for name, a in arrays.items()}
    out = nc.dram_tensor("scores_dram", (1, BATCH), mybir.dt.float32, kind="ExternalOutput").ap()
    nnue_kernel(nc, args["indices"], args["tables"], args["ft_w"], args["w1"], args["w2"], args["w3"],
                args["biases"], args["bo"], out)
    result = run_bass_kernel_spmd(nc, [{f"{name}_dram": a for name, a in arrays.items()}], core_ids=[0])
    return result.results[0]["scores_dram"].reshape(BATCH)
```

```python
import concourse.bass as bass
from concourse import mybir
from contextlib import ExitStack

SIDES = 2
ACTIVE = 30
FEATURES = 4476
HIDDEN = 512
BATCH = 2048
TILE = 128
HIGHS = -(-FEATURES // TILE)
PADDED = HIGHS * TILE
CHUNK = 512
PAIRS = BATCH // CHUNK
ROWS = 4
CHAINS = 3
GATHERED = CHAINS * TILE // SIDES
COUNTED = CHUNK - GATHERED
QUADS = COUNTED // ROWS
ALL_QUADS = SIDES * PAIRS * QUADS
INDEX_PART = (ALL_QUADS - QUADS) // 2
PAIRS_OF_INDICES = ROWS * ACTIVE
GROUP = 4
GROUPS = QUADS // GROUP
COUNTS = HIGHS * ROWS
COUNT_STRIDE = 256
UNIT_TILES = HIDDEN // TILE
SECTIONS = 5
SECTION = HIGHS // SECTIONS
SECTION_COLUMNS = SECTION * TILE
RING = 5
H1 = 512
H2 = 256
H3 = 128
MAX_FLOAT_EXPONENT_PAIR = 254
SCALED_EXPONENT = 14


def nnue_kernel(nc, indices, gather_indices, code_table, unit_matrix, ft_w, feature_rows, w1, w2, w3, biases, bo, out):
    F32, F16, I32 = mybir.dt.float32, mybir.dt.float16, mybir.dt.int32
    ALU, ACT, AX = mybir.AluOpType, mybir.ActivationFunctionType, mybir.AxisListType

    ctx = ExitStack()
    with ctx:
        def sb(name, shape, dt):
            return ctx.enter_context(nc.sbuf_tensor(name, shape, dt))

        def pb(name, shape, dt):
            return ctx.enter_context(nc.psum_tensor(name, shape, dt))

        def sem(name):
            return ctx.enter_context(nc.semaphore(name))

        weights = sb("weights", [TILE, 2, HIGHS, HIDDEN], F16)
        multihot_region = sb("multihot_region", [TILE, (HIGHS * COUNTED * (SIDES - 1) + 2 * 2 * PADDED)], F16)
        multihot = [multihot_region[:, HIGHS * COUNTED * i:HIGHS * COUNTED * (i + 1)]
                    .rearrange("p (k n) -> p k n", n=COUNTED) for i in range(SIDES)]
        mlp_region = sb("mlp_region", [TILE, 8 * H1 + 4 * H2 + 2 * H3], F32)
        hidden_region = sb("hidden_region", [TILE, H1 // TILE + SIDES * UNIT_TILES, CHUNK], F32)
        hidden1 = hidden_region[:, 0:H1 // TILE, :]
        hidden0 = hidden_region[:, H1 // TILE:, :]
        small_region = sb("small_region", [TILE, 2 * 2 * SECTION_COLUMNS], F16)
        high_hot = sb("high_hot", [PAIRS_OF_INDICES, RING, COUNTS, GROUP], F16)
        low_hot = sb("low_hot", [PAIRS_OF_INDICES, RING, TILE, GROUP], F16)
        high = sb("high", [PAIRS_OF_INDICES, ALL_QUADS], F16)
        low = sb("low", [PAIRS_OF_INDICES, ALL_QUADS], F16)
        codes = sb("codes", [PAIRS_OF_INDICES, COUNTS + TILE, GROUP], F16)
        high_codes = codes[:, 0:COUNTS, :]
        low_codes = codes[:, COUNTS:COUNTS + TILE, :]
        largest = sb("largest", [TILE, UNIT_TILES], F32)
        power = sb("power", [TILE, UNIT_TILES], I32)
        unscale = sb("unscale", [TILE, UNIT_TILES], F32)
        scale = sb("scale", [TILE, UNIT_TILES], F32)
        bias = sb("bias", [TILE, 8], F32)
        bias_out = sb("bias_out", [1, 1], F32)
        listed = sb("listed", [TILE, PAIRS, CHAINS, ACTIVE], I32)
        equal = sb("equal", [TILE, CHAINS, ACTIVE, ACTIVE - 1], F16)
        repeated = sb("repeated", [TILE, CHAINS, ACTIVE], F16)
        rows_wanted = sb("rows_wanted", [TILE, CHAINS, ACTIVE], I32)
        sums = [sb(f"sums{chain}", [TILE, HIDDEN], F32) for chain in range(CHAINS)]
        unit_matrix32 = sb("unit_matrix32", [TILE, TILE], F32)

        hidden_words = hidden_region[:, :, :].rearrange("p k n -> p (k n)")
        stages = [hidden_words[:, hidden_words.shape[1] - PADDED:]]
        stages += [multihot_region[:, HIGHS * COUNTED + 2 * PADDED * i:HIGHS * COUNTED + 2 * PADDED * (i + 1)]
                   .bitcast(F32) for i in range(2)]
        stages += [mlp_region[:, 0:PADDED]]
        w1_sb = mlp_region[:, 0:8 * H1].rearrange("p (k n) -> p k n", n=H1)
        w2_sb = mlp_region[:, 8 * H1:8 * H1 + 4 * H2].rearrange("p (k n) -> p k n", n=H2)
        w3_sb = mlp_region[:, 8 * H1 + 4 * H2:].rearrange("p (k n) -> p k n", n=H3)
        index = hidden_words[0:PAIRS_OF_INDICES, 0:ALL_QUADS].bitcast(I32)
        high_int = hidden_words[0:PAIRS_OF_INDICES, ALL_QUADS:ALL_QUADS + INDEX_PART].bitcast(I32)
        identity_at = hidden_words.shape[1] - PADDED - TILE // 2
        identity = hidden_words[:, identity_at:identity_at + TILE // 2].bitcast(F16)
        assert ALL_QUADS + INDEX_PART <= identity_at and identity_at + TILE // 2 <= H1 // TILE * CHUNK
        split = small_region[:, :].rearrange("p (s h n) -> p s h n", s=2, h=2)
        hidden2 = small_region[:, 0:2 * 2 * CHUNK].bitcast(F32).rearrange("p (k n) -> p k n", n=CHUNK)
        hidden3 = small_region[:, 4 * CHUNK:6 * CHUNK].bitcast(F32)
        scores = hidden2[0:1, 0, :]

        transform_banks = pb("transform", [TILE, 2, CHUNK], F32)
        transform = transform_banks[:, :, 0:COUNTED]
        counts = pb("counts", [TILE, 2, GROUP, COUNT_STRIDE], F32)
        layer = pb("layer", [TILE, 2, CHUNK], F32)
        turned = [layer[:, i, :].bitcast(F16)[:, 0:SECTION_COLUMNS] for i in range(2)]

        index_loaded = sem("index_loaded")
        codes_loaded = sem("codes_loaded")
        identity_loaded = sem("identity_loaded")
        stage_loaded = [sem(f"stage{m}_loaded") for m in range(UNIT_TILES)]
        mlp_loaded = sem("mlp_loaded")
        bias_loaded = sem("bias_loaded")
        pad_cleared = sem("pad_cleared")
        index_steps = sem("index_steps")
        onehots_ready = sem("onehots_ready")
        counted = sem("counted")
        multihot_ready = sem("multihot_ready")
        scale_steps = sem("scale_steps")
        listed_loaded = sem("listed_loaded")
        equal_cleared = sem("equal_cleared")
        repeat_steps = sem("repeat_steps")
        rows_ready = sem("rows_ready")
        gathered = [sem(f"gathered{chain}") for chain in range(CHAINS)]
        sums_turned = sem("sums_turned")
        sums_clipped = sem("sums_clipped")
        high_split = sem("high_split")
        low_split = sem("low_split")
        high_turned = sem("high_turned")
        low_turned = sem("low_turned")
        high_placed = sem("high_placed")
        low_placed = sem("low_placed")
        transform_done = sem("transform_done")
        transform_read = sem("transform_read")
        hidden0_ready = sem("hidden0_ready")
        layer_done = sem("layer_done")
        layer_read = sem("layer_read")
        stored = sem("stored")

        LAYER_BANKS = H1 // TILE + H2 // TILE + H3 // TILE + 1
        block = ctx.enter_context(nc.Block())

        @block.sync
        def _(sp):
            sp.dma_start(index, indices).then_inc(index_loaded, 16)
            for m in range(UNIT_TILES):
                sp.dma_start(stages[m][:, 0:FEATURES], ft_w[m * TILE:(m + 1) * TILE, :])\
                    .then_inc(stage_loaded[m], 16)
            sp.dma_start(listed[:, :, :, :], gather_indices).then_inc(listed_loaded, 16)
            sp.wait_ge(high_split, UNIT_TILES * SECTIONS)
            sp.wait_ge(low_split, UNIT_TILES * SECTIONS)
            sp.dma_start(w1_sb, w1).then_inc(mlp_loaded, 16)
            sp.dma_start(w2_sb, w2).then_inc(mlp_loaded, 16)
            sp.dma_start(w3_sb, w3).then_inc(mlp_loaded, 16)

            with sp.Fori(0, PAIRS) as pair:
                sp.wait_ge(layer_read, LAYER_BANKS * pair + LAYER_BANKS)
                sp.dma_start(out[0:1, bass.ds(pair * CHUNK, CHUNK)], scores).then_inc(stored, 16)
            sp.wait_ge(stored, 16 * PAIRS)

        @block.gpsimd
        def _(pool):
            for stage in stages:
                nc.gpsimd.memset(stage[:, FEATURES:PADDED], 0.0).then_inc(pad_cleared, 1)
            nc.gpsimd.memset(equal[:, :, :, :], 0.0).then_inc(equal_cleared, 1)
            nc.gpsimd.memset(unit_matrix32[:, :], 0.0).then_inc(equal_cleared, 1)
            pool.wait_ge(equal_cleared, 2)
            nc.gpsimd.affine_select(out=unit_matrix32[:, :], in_=unit_matrix32[:, :], compare_op=ALU.not_equal,
                                    fill=1.0, base=0, pattern=[[-1, TILE]], channel_multiplier=1)\
                .then_inc(equal_cleared, 1)

            with pool.Fori(0, PAIRS) as pair:
                pool.wait_ge(rows_ready, pair + 1)
                for j in range(ACTIVE):
                    for chain in range(CHAINS):
                        if j:
                            pool.wait_ge(gathered[chain], 16 * ACTIVE * pair + 16 * j)
                        pool.nop(nofuse=True)
                        nc.gpsimd.indirect_dma_start(
                            out=sums[chain][:, :], out_offset=None, in_=feature_rows,
                            in_offset=bass.IndirectOffsetOnAxis(ap=rows_wanted[:, chain, j:j + 1], axis=0),
                            compute_op=ALU.add if j else ALU.bypass).then_inc(gathered[chain], 16)

        @block.vector
        def _(dve):
            def split_indices(part, first, size):
                quads = slice(first, first + size)
                to = slice(0, size)
                nc.vector.tensor_scalar(high_int[:, to], index[:, quads], 7, None,
                                        ALU.arith_shift_right).then_inc(index_steps, 1)
                dve.wait_ge(index_steps, 3 * part + 1)
                nc.vector.tensor_copy(high[:, quads], high_int[:, to]).then_inc(index_steps, 1)
                dve.wait_ge(index_steps, 3 * part + 2)
                nc.vector.scalar_tensor_tensor(out=low[:, quads], in0=high[:, quads], scalar=-float(TILE),
                                               in1=index[:, quads], op0=ALU.mult, op1=ALU.add)\
                    .then_inc(index_steps, 1)
                dve.wait_ge(index_steps, 3 * part + 3)

            def compare(group, slot, ring_full=True):
                if ring_full:
                    dve.wait_ge(counted, group - (RING - 1))
                quads = bass.ds(group * GROUP, GROUP)
                nc.vector.tensor_tensor(
                    high_hot[:, slot, :, :], high_codes,
                    high[:, quads].unsqueeze(1).to_broadcast([PAIRS_OF_INDICES, COUNTS, GROUP]), ALU.is_equal)
                nc.vector.tensor_tensor(
                    low_hot[:, slot, :, :], low_codes,
                    low[:, quads].unsqueeze(1).to_broadcast([PAIRS_OF_INDICES, TILE, GROUP]), ALU.is_equal)\
                    .then_inc(onehots_ready, 1)

            def weight_scale(m):
                dve.wait_ge(stage_loaded[m], 16)
                dve.wait_ge(pad_cleared, m + 1)
                column = slice(m, m + 1)
                nc.vector.tensor_reduce(largest[:, column], stages[m][:, :], AX.X, ALU.max,
                                        apply_absolute_value=True).then_inc(scale_steps, 1)
                dve.wait_ge(scale_steps, 4 * m + 1)
                nc.vector.tensor_scalar(power[:, column], largest[:, column].bitcast(I32), 0xFF << 23, None,
                                        ALU.bitwise_and).then_inc(scale_steps, 1)
                dve.wait_ge(scale_steps, 4 * m + 2)
                nc.vector.tensor_scalar(unscale[:, column].bitcast(I32), power[:, column],
                                        float((SCALED_EXPONENT + 1) << 23), float(SCALED_EXPONENT << 23),
                                        ALU.max, ALU.subtract).then_inc(scale_steps, 1)
                dve.wait_ge(scale_steps, 4 * m + 3)
                nc.vector.tensor_scalar(scale[:, column].bitcast(I32), unscale[:, column].bitcast(I32),
                                        -1.0, float(MAX_FLOAT_EXPONENT_PAIR << 23),
                                        ALU.mult, ALU.add).then_inc(scale_steps, 1)
                dve.wait_ge(scale_steps, 4 * m + 4)

            def split_low(n):
                m, s = divmod(n, SECTIONS)
                dve.wait_ge(high_split, n + 1)
                if n >= 2:
                    dve.wait_ge(low_turned, n - 1)
                nc.vector.scalar_tensor_tensor(
                    out=split[:, n % 2, 1, :], in0=stages[m][:, s * SECTION_COLUMNS:(s + 1) * SECTION_COLUMNS],
                    scalar=scale[:, m:m + 1], in1=split[:, n % 2, 0, :],
                    op0=ALU.mult, op1=ALU.subtract).then_inc(low_split, 1)

            def place_low(n):
                m, s = divmod(n, SECTIONS)
                dve.wait_ge(low_turned, n + 1)
                nc.vector.tensor_copy(weights[:, 1, s * SECTION:(s + 1) * SECTION, m * TILE:(m + 1) * TILE],
                                      turned[1].rearrange("p (k n) -> p k n", n=TILE))\
                    .then_inc(low_placed, 1)

            def find_rows(pair):
                for d in range(1, ACTIVE):
                    last = nc.vector.tensor_tensor(
                        equal[:, :, d:ACTIVE, d - 1], listed[:, bass.ds(pair, 1), :, d:ACTIVE].squeeze(1),
                        listed[:, bass.ds(pair, 1), :, 0:ACTIVE - d].squeeze(1), ALU.is_equal)
                last.then_inc(repeat_steps, 1)
                dve.wait_ge(repeat_steps, 2 * pair + 1)
                nc.vector.tensor_reduce(repeated[:, :, :], equal[:, :, :, :], AX.X, ALU.max)\
                    .then_inc(repeat_steps, 1)
                dve.wait_ge(repeat_steps, 2 * pair + 2)
                nc.vector.scalar_tensor_tensor(
                    out=rows_wanted[:, :, :], in0=repeated[:, :, :], scalar=float(FEATURES),
                    in1=listed[:, bass.ds(pair, 1), :, :].squeeze(1), op0=ALU.mult, op1=ALU.max)\
                    .then_inc(rows_ready, 1)

            def clip_sums(pair):
                for chain in range(CHAINS):
                    dve.wait_ge(sums_turned, CHAINS * pair + chain + 1)
                    if chain < SIDES:
                        to = hidden0[:, UNIT_TILES * chain:UNIT_TILES * (chain + 1), COUNTED:COUNTED + TILE]
                        units = layer[:, chain, :].rearrange("p (m n) -> p m n", n=TILE)
                    else:
                        to = hidden0[:, :, COUNTED + TILE:CHUNK].rearrange("p (s m) n -> p s m n", s=SIDES)
                        units = layer[:, 0, :].rearrange("p (m s n) -> p s m n", s=SIDES, m=UNIT_TILES)
                    nc.vector.tensor_scalar(to, units, 1.0, -1.0, ALU.min, ALU.max).then_inc(sums_clipped, 1)

            def clip(unit_tile, bank, row, m):
                dve.wait_ge(transform_done, unit_tile + 1)
                nc.vector.tensor_scalar(hidden0[:, row, 0:COUNTED], transform[:, bank, :],
                                        unscale[:, bass.ds(m, 1)], 1.0, ALU.mult, ALU.min)\
                    .then_inc(transform_read, 1)
                dve.wait_ge(transform_read, unit_tile + 1)
                nc.vector.tensor_scalar(hidden0[:, row, 0:COUNTED], hidden0[:, row, 0:COUNTED], -1.0, None, ALU.max)\
                    .then_inc(hidden0_ready, 1)

            dve.wait_ge(index_loaded, 16)
            split_indices(0, 0, QUADS)
            dve.wait_ge(codes_loaded, 16)
            for g in range(EARLY_GROUPS):
                compare(g, g % RING, g >= RING)
            weight_scale(0)
            split_low(0)
            for s in range(SECTIONS):
                for g in second_groups(s):
                    compare(g, g % RING)
                if s + 1 < SECTIONS:
                    split_low(s + 1)
                if s > 0:
                    place_low(s - 1)
            for s in range(SECTIONS):
                for g in third_groups(s):
                    compare(g, g % RING)
                if s == HALF_FROM:
                    place_low(SECTIONS - 1)
            weight_scale(1)
            split_low(SECTIONS)
            dve.wait_ge(listed_loaded, 16)
            dve.wait_ge(equal_cleared, 1)
            find_rows(0)
            for n in range(UNIT_TILES * SECTIONS):
                m, s = divmod(n, SECTIONS)
                if n in SCALES:
                    weight_scale(SCALES[n])
                for g in first_chunk_groups(n):
                    compare(GROUPS + g, g % RING)
                for t in turned_after(n):
                    if t + 1 < UNIT_TILES * SECTIONS:
                        split_low(t + 1)
                    place_low(t)
                if n == SECTIONS - 1:
                    split_indices(1, QUADS, INDEX_PART)
                    split_indices(2, QUADS + INDEX_PART, INDEX_PART)
                if s == SECTIONS - 1:
                    clip(m, m % 2, m, m)

            def products_of(chunk, side):
                with dve.Fori(0, UNIT_TILES // 2) as half:
                    for parity in range(2):
                        m = 2 * half + parity
                        for j in range(TILE_GROUPS * parity, TILE_GROUPS * (parity + 1)):
                            compare(GROUPS * chunk + GROUPS + 2 * TILE_GROUPS * half + j, j % RING)
                        clip(UNIT_TILES * chunk + m, parity, UNIT_TILES * side + m, m)

            with dve.Fori(0, PAIRS - 1) as pair:
                products_of(2 * pair + 1, 1)
                clip_sums(pair)
                find_rows(pair + 1)
                products_of(2 * pair + 2, 0)
            for m in range(UNIT_TILES):
                clip(UNIT_TILES * (2 * PAIRS - 1) + m, m % 2, UNIT_TILES + m, m)
            clip_sums(PAIRS - 1)

        @block.scalar
        def _(act):
            act.dma_start(codes[:, :, :], code_table).then_inc(codes_loaded, 16)
            act.dma_start(identity, unit_matrix).then_inc(identity_loaded, 16)
            act.dma_start(bias[:, :], biases).then_inc(bias_loaded, 16)
            act.dma_start(bias_out[:, :], bo).then_inc(bias_loaded, 16)

            def place_multihot(group, bank, quad_columns, side):
                act.wait_ge(counted, group + 1)
                nc.scalar.activation(
                    multihot[side][:, :, quad_columns].rearrange("p h (q b) -> p h q b", b=ROWS),
                    counts[:, bank, :, 0:COUNTS].rearrange("p q (h b) -> p h q b", b=ROWS),
                    ACT.Sign).then_inc(multihot_ready, 1)

            def split_high(n):
                m, s = divmod(n, SECTIONS)
                if s == 0:
                    act.wait_ge(scale_steps, 4 * m + 4)
                if n >= 2:
                    act.wait_ge(low_split, n - 1)
                    act.wait_ge(high_turned, n - 1)
                columns = slice(s * SECTION_COLUMNS, (s + 1) * SECTION_COLUMNS)
                nc.scalar.activation(split[:, n % 2, 0, :], stages[m][:, columns], ACT.Copy,
                                     scale=scale[:, m:m + 1]).then_inc(high_split, 1)

            def place_high(n):
                m, s = divmod(n, SECTIONS)
                act.wait_ge(high_turned, n + 1)
                nc.scalar.activation(weights[:, 0, s * SECTION:(s + 1) * SECTION, m * TILE:(m + 1) * TILE],
                                     turned[0].rearrange("p (k n) -> p k n", n=TILE), ACT.Copy)\
                    .then_inc(high_placed, 1)

            def columns_of(g):
                return slice(g * GROUP * ROWS, (g + 1) * GROUP * ROWS)

            def columns_at(g):
                return bass.ds(g * (GROUP * ROWS), GROUP * ROWS)

            for g in range(EARLY_GROUPS):
                place_multihot(g, g % 2, columns_of(g), 0)
            split_high(0)
            split_high(1)
            for s in range(SECTIONS):
                place_high(s)
                if s + 2 < SECTIONS:
                    split_high(s + 2)
                for g in second_groups(s):
                    place_multihot(g, g % 2, columns_of(g), 0)
            for s in range(SECTIONS):
                for g in third_groups(s):
                    place_multihot(g, g % 2, columns_of(g), 0)
            split_high(SECTIONS)
            split_high(SECTIONS + 1)
            for n in range(UNIT_TILES * SECTIONS):
                groups = first_chunk_groups(n)
                if groups and groups[0] == 0:
                    act.wait_ge(low_split, 3 * SECTIONS)
                for g in groups:
                    place_multihot(GROUPS + g, g % 2, columns_of(g), 1)
                for t in turned_after(n):
                    place_high(t)
                    if t + 2 < UNIT_TILES * SECTIONS:
                        split_high(t + 2)

            def place_groups(first_group, side):
                with act.Fori(0, UNIT_TILES // 2) as half:
                    for j in range(2 * TILE_GROUPS):
                        g = 2 * TILE_GROUPS * half + j
                        place_multihot(first_group + g, j % 2, columns_at(g), side)

            def relu_bank(pair, bank_number, to):
                act.wait_ge(layer_done, LAYER_BANKS * pair + bank_number + 1)
                nc.scalar.activation(to, layer[:, bank_number % 2, :], ACT.Relu,
                                     bias=bias[:, bank_number:bank_number + 1]).then_inc(layer_read, 1)

            def relu_layers(pair):
                for t in range(H1 // TILE):
                    relu_bank(pair, t, hidden1[:, t, :])
                for t in range(H2 // TILE):
                    relu_bank(pair, 4 + t, hidden2[:, t, :])
                relu_bank(pair, 6, hidden3)

            def score(pair):
                act.wait_ge(layer_done, LAYER_BANKS * pair + LAYER_BANKS)
                nc.scalar.activation(scores, layer[0:1, 1, :], ACT.Identity, bias=bias_out[:, :])\
                    .then_inc(layer_read, 1)

            act.wait_ge(bias_loaded, 32)
            with act.Fori(0, PAIRS - 1) as pair:
                place_groups(GROUPS * (2 * pair + 2), 0)
                relu_layers(pair)
                place_groups(GROUPS * (2 * pair + 3), 1)
                score(pair)
                act.wait_ge(stored, 16 * pair + 16)
            relu_layers(PAIRS - 1)
            score(PAIRS - 1)

        @block.tensor
        def _(pe):
            def count(group, slot, bank, first=False):
                pe.wait_ge(onehots_ready, group + 1)
                if not first:
                    pe.wait_ge(multihot_ready, group - 1)
                for q in range(GROUP):
                    last = nc.tensor.matmul(counts[:, bank, q, 0:COUNTS], low_hot[:, slot, :, q],
                                            high_hot[:, slot, :, q], start=True, stop=True)
                last.then_inc(counted, 1)

            def turn(n):
                for part, was_placed, was_turned in ((0, high_placed, high_turned), (1, low_placed, low_turned)):
                    if part == 0:
                        pe.wait_ge(high_split, n + 1)
                    else:
                        pe.wait_ge(low_split, n + 1)
                    if n:
                        pe.wait_ge(was_placed, n)
                    for k in range(SECTION):
                        last = nc.tensor.transpose(turned[part][:, k * TILE:(k + 1) * TILE],
                                                   split[:, n % 2, part, k * TILE:(k + 1) * TILE],
                                                   identity)
                    last.then_inc(was_turned, 1)

            def multiply(side, units, bank, s, positions=slice(0, COUNTED), between=()):
                between = list(between)
                for k in range(s * SECTION, (s + 1) * SECTION):
                    for part in range(2):
                        last = nc.tensor.matmul(transform[:, bank, positions], weights[:, part, k, units],
                                                multihot[side][:, k, positions],
                                                start=(k == 0 and part == 0),
                                                stop=(k == HIGHS - 1 and part == 1))
                    if between and (k - s * SECTION) % 2 == 1:
                        count(*between.pop(0))
                for group in between:
                    count(*group)
                return last

            for g in range(EARLY_GROUPS):
                count(g, g % RING, g % 2, first=g < 2)
            pe.wait_ge(identity_loaded, 16)
            first_half = slice(0, COUNTED // 2)
            second_half = slice(COUNTED // 2, COUNTED)

            def multiply_first_half(s):
                if s == 0:
                    pe.wait_ge(multihot_ready, GROUPS // 2)
                pe.wait_ge(high_placed, s + 1)
                pe.wait_ge(low_placed, s + 1)
                multiply(0, slice(0, TILE), 0, s, first_half, [(g, g % RING, g % 2) for g in third_groups(s)])

            for s in range(SECTIONS):
                turn(s)
                for g in second_groups(s):
                    count(g, g % RING, g % 2)
                if s >= SECTIONS - HALF_FROM:
                    multiply_first_half(s - (SECTIONS - HALF_FROM))
            for s in range(HALF_FROM, SECTIONS):
                multiply_first_half(s)
            pe.wait_ge(multihot_ready, GROUPS)
            for n in range(UNIT_TILES * SECTIONS):
                m, s = divmod(n, SECTIONS)
                if m >= 2 and s == 0:
                    pe.wait_ge(transform_read, m - 1)
                if m > 0:
                    pe.wait_ge(high_placed, n + 1)
                    pe.wait_ge(low_placed, n + 1)
                last = multiply(0, slice(m * TILE, (m + 1) * TILE), m % 2, s,
                                slice(0, COUNTED) if m > 0 else second_half,
                                [(GROUPS + g, g % RING, g % 2) for g in first_chunk_groups(n)])
                if s == SECTIONS - 1:
                    last.then_inc(transform_done, 1)
                for t in turned_after(n):
                    turn(t)

            def multiply_chunk(chunk, side):
                with pe.Fori(0, UNIT_TILES // 2) as half:
                    pe.wait_ge(multihot_ready, GROUPS * chunk + GROUPS)
                    for parity in range(2):
                        m = 2 * half + parity
                        pe.wait_ge(transform_read, UNIT_TILES * chunk + m - 1)
                        counts_made = 0
                        for s in range(SECTIONS):
                            last = multiply(side, bass.ds(m * TILE, TILE), parity, s)
                            if s == SECTIONS - 1:
                                last.then_inc(transform_done, 1)
                            while counts_made < TILE_GROUPS * (s + 1) // SECTIONS:
                                j = TILE_GROUPS * parity + counts_made
                                count(GROUPS * chunk + GROUPS + 2 * TILE_GROUPS * half + j, j % RING, j % 2)
                                counts_made += 1

            def dense(pair, bank_number, weight, activation, inputs_ready, before):
                tiles = len(weight)
                pe.wait_ge(inputs_ready, before)
                for k in range(tiles):
                    if k == tiles - 1:
                        pe.wait_ge(inputs_ready, before + 1)
                    last = nc.tensor.matmul(layer[:, bank_number % 2, :], weight[k], activation[:, k, :],
                                            start=(k == 0), stop=(k == tiles - 1))
                last.then_inc(layer_done, 1)

            def turn_sums(pair):
                for chain in range(CHAINS):
                    pe.wait_ge(gathered[chain], 16 * ACTIVE * pair + 16 * ACTIVE)
                    if chain == 2:
                        pe.wait_ge(sums_clipped, CHAINS * pair + 1)
                    for m in range(UNIT_TILES):
                        last = nc.tensor.transpose(layer[:, chain % 2, m * TILE:(m + 1) * TILE],
                                                   sums[chain][:, m * TILE:(m + 1) * TILE], unit_matrix32[:, :])
                    last.then_inc(sums_turned, 1)

            def later_layers(pair):
                banks = LAYER_BANKS * pair
                pe.wait_ge(sums_clipped, CHAINS * pair + CHAINS)
                for t in range(H1 // TILE):
                    if t >= 2:
                        pe.wait_ge(layer_read, banks + t - 1)
                    dense(pair, t, [w1_sb[:, k, t * TILE:(t + 1) * TILE] for k in range(SIDES * UNIT_TILES)],
                          hidden0, hidden0_ready, SIDES * UNIT_TILES * pair + 7)
                for t in range(H2 // TILE):
                    if t == 1:
                        pe.wait_ge(layer_read, banks + 4)
                    dense(pair, 4 + t, [w2_sb[:, k, t * TILE:(t + 1) * TILE] for k in range(H1 // TILE)],
                          hidden1, layer_read, banks + 3)
                dense(pair, 6, [w3_sb[:, k, :] for k in range(H2 // TILE)], hidden2, layer_read, banks + 5)

            def output_layer(pair):
                pe.wait_ge(layer_read, LAYER_BANKS * pair + 7)
                nc.tensor.matmul(layer[0:1, 1, :], bias[:, 7:8], hidden3, start=True, stop=True)\
                    .then_inc(layer_done, 1)

            pe.wait_ge(mlp_loaded, 48)
            pe.wait_ge(equal_cleared, 3)
            pe.wait_ge(bias_loaded, 32)
            with pe.Fori(0, PAIRS - 1) as pair:
                multiply_chunk(2 * pair + 1, 1)
                turn_sums(pair)
                later_layers(pair)
                multiply_chunk(2 * pair + 2, 0)
                output_layer(pair)
            pe.wait_ge(layer_read, LAYER_BANKS * (PAIRS - 1))
            pe.wait_ge(multihot_ready, GROUPS * SIDES * PAIRS)
            for m in range(UNIT_TILES):
                pe.wait_ge(transform_read, UNIT_TILES * (SIDES * PAIRS - 1) + m - 1)
                for s in range(SECTIONS):
                    last = multiply(1, slice(m * TILE, (m + 1) * TILE), m % 2, s)
                last.then_inc(transform_done, 1)
            turn_sums(PAIRS - 1)
            later_layers(PAIRS - 1)
            output_layer(PAIRS - 1)


TILE_GROUPS = GROUPS // UNIT_TILES
assert 2 * TILE_GROUPS % RING == 0
EARLY_GROUPS = 8
LATE_GROUPS = EARLY_GROUPS + 2 * SECTIONS


def second_groups(s):
    return range(EARLY_GROUPS + 2 * s, EARLY_GROUPS + 2 * s + 2)


def third_groups(s):
    if s < HALF_FROM:
        return range(0)
    rest, steps, s = GROUPS - LATE_GROUPS, SECTIONS - HALF_FROM, s - HALF_FROM
    return range(LATE_GROUPS + rest * s // steps, LATE_GROUPS + rest * (s + 1) // steps)


HALF_FROM = 3
SCALES = {1: 2, 8: 3}


def turned_after(n):
    def through(n):
        return max(SECTIONS, min(UNIT_TILES * SECTIONS, n + 3 + (n >= 7) + (n >= 9)))
    return range(through(n - 1), through(n))


def first_chunk_groups(n):
    first, last = 11, UNIT_TILES * SECTIONS
    if n < first:
        return range(0)
    return range(GROUPS * (n - first) // (last - first), GROUPS * (n - first + 1) // (last - first))


def kernel(**inputs):
    import numpy as np
    import concourse.bacc as bacc
    from concourse.bass_utils import run_bass_kernel_spmd

    def counted(name):
        a = np.asarray(inputs[name]).reshape(PAIRS, CHUNK, ACTIVE)[:, :COUNTED]
        a = a.reshape(PAIRS, QUADS, ROWS, ACTIVE)
        return a.transpose(2, 3, 0, 1).reshape(PAIRS_OF_INDICES, PAIRS, QUADS)

    def gathered(name):
        return np.asarray(inputs[name]).reshape(PAIRS, CHUNK, ACTIVE)[:, COUNTED:].transpose(1, 0, 2)

    white, black = gathered("r_white_indices"), gathered("r_black_indices")
    chains = [white[:TILE], black[:TILE], np.concatenate([white[TILE:], black[TILE:]])]

    def both(side):
        return np.ascontiguousarray(np.stack([side("r_white_indices"), side("r_black_indices")], axis=2))

    def tiled(name):
        a = np.asarray(inputs["L0_rec_" + name]).T
        return np.ascontiguousarray(a.reshape(-1, TILE, a.shape[1]).transpose(1, 0, 2))

    def columns(name):
        return np.asarray(inputs["L0_rec_" + name]).reshape(-1, TILE).T

    owner = np.arange(PAIRS_OF_INDICES)[:, None, None] // ACTIVE
    high_codes = np.where(np.arange(ROWS)[None, None, :] == owner, np.arange(HIGHS)[None, :, None], -1)
    low_codes = np.broadcast_to(np.arange(TILE), (PAIRS_OF_INDICES, TILE))
    codes = np.concatenate([high_codes.reshape(PAIRS_OF_INDICES, COUNTS), low_codes], axis=1)

    arrays = {
        "indices": both(counted).reshape(PAIRS_OF_INDICES, ALL_QUADS),
        "gather_indices": np.ascontiguousarray(np.stack(chains, axis=2)),
        "codes": np.repeat(codes[:, :, None], GROUP, axis=2).astype(np.float16),
        "identity": np.eye(TILE, dtype=np.float16),
        "ft_w": np.ascontiguousarray(inputs["L0_rec_ft_w"]),
        "feature_rows": np.pad(np.asarray(inputs["L0_rec_ft_w"]).T, ((0, 1), (0, 0))),
        "w1": tiled("w1"), "w2": tiled("w2"), "w3": tiled("w3"),
        "biases": np.ascontiguousarray(np.concatenate(
            [columns("b1"), columns("b2"), columns("b3"), columns("wo")], axis=1)),
        "bo": np.asarray(inputs["L0_rec_bo"]).reshape(1, 1),
    }
    nc = bacc.Bacc("TRN2", target_bir_lowering=False, num_devices=1)
    args = {name: nc.dram_tensor(f"{name}_dram", a.shape, mybir.dt.from_np(a.dtype), kind="ExternalInput").ap()
            for name, a in arrays.items()}
    out = nc.dram_tensor("scores_dram", (1, BATCH), mybir.dt.float32, kind="ExternalOutput").ap()
    nnue_kernel(nc, *args.values(), out)
    result = run_bass_kernel_spmd(nc, [{f"{name}_dram": a for name, a in arrays.items()}], core_ids=[0])
    return result.results[0]["scores_dram"].reshape(BATCH)
```

```python
import concourse.bass as bass
from concourse import mybir
from contextlib import ExitStack

SIDES = 2
ACTIVE = 30
FEATURES = 4476
HIDDEN = 512
BATCH = 2048
TILE = 128
HIGHS = -(-FEATURES // TILE)
PADDED = HIGHS * TILE
CHUNK = 512
PAIRS = BATCH // CHUNK
ROWS = 4
CHAINS = 3
GATHERED = CHAINS * TILE // SIDES
COUNTED = CHUNK - GATHERED
QUADS = COUNTED // ROWS
ALL_QUADS = SIDES * PAIRS * QUADS
INDEX_PART = (ALL_QUADS - QUADS) // 2
PAIRS_OF_INDICES = ROWS * ACTIVE
GROUP = 4
GROUPS = QUADS // GROUP
COUNTS = HIGHS * ROWS
COUNT_STRIDE = 256
UNIT_TILES = HIDDEN // TILE
SECTIONS = 5
SECTION = HIGHS // SECTIONS
SECTION_COLUMNS = SECTION * TILE
RING = 5
H1 = 512
H2 = 256
H3 = 128
MAX_FLOAT_EXPONENT_PAIR = 254
SCALED_EXPONENT = 14


def nnue_kernel(nc, indices, gather_indices, code_table, unit_matrix, ft_w, feature_rows, w1, w2, w3,
                biases, bo, out):
    F32, F16, I32 = mybir.dt.float32, mybir.dt.float16, mybir.dt.int32
    ALU, ACT, AX = mybir.AluOpType, mybir.ActivationFunctionType, mybir.AxisListType

    ctx = ExitStack()
    with ctx:
        def sb(name, shape, dt):
            return ctx.enter_context(nc.sbuf_tensor(name, shape, dt))

        def pb(name, shape, dt):
            return ctx.enter_context(nc.psum_tensor(name, shape, dt))

        def sem(name):
            return ctx.enter_context(nc.semaphore(name))

        weights = sb("weights", [TILE, 2, HIGHS, HIDDEN], F16)
        multihot_region = sb("multihot_region", [TILE, HIGHS * COUNTED + 2 * 2 * PADDED], F16)
        multihot = [multihot_region[:, HIGHS * COUNTED * i:HIGHS * COUNTED * (i + 1)]
                    .rearrange("p (k n) -> p k n", n=COUNTED) for i in range(SIDES)]
        mlp_region = sb("mlp_region", [TILE, 8 * H1 + 4 * H2 + 2 * H3], F32)
        hidden_region = sb("hidden_region", [TILE, H1 // TILE + SIDES * UNIT_TILES, CHUNK], F32)
        hidden1 = hidden_region[:, 0:H1 // TILE, :]
        hidden0 = hidden_region[:, H1 // TILE:, :]
        small_region = sb("small_region", [TILE, 2 * 2 * SECTION_COLUMNS], F16)
        high_hot = sb("high_hot", [PAIRS_OF_INDICES, RING, COUNTS, GROUP], F16)
        low_hot = sb("low_hot", [PAIRS_OF_INDICES, RING, TILE, GROUP], F16)
        high = sb("high", [PAIRS_OF_INDICES, ALL_QUADS], F16)
        low = sb("low", [PAIRS_OF_INDICES, ALL_QUADS], F16)
        codes = sb("codes", [PAIRS_OF_INDICES, COUNTS + TILE, GROUP], F16)
        high_codes = codes[:, 0:COUNTS, :]
        low_codes = codes[:, COUNTS:COUNTS + TILE, :]
        section_largest = sb("section_largest", [TILE, UNIT_TILES, SECTIONS], F32)
        largest = sb("largest", [TILE, UNIT_TILES], F32)
        power = sb("power", [TILE, UNIT_TILES], I32)
        unscale = sb("unscale", [TILE, UNIT_TILES], F32)
        scale = sb("scale", [TILE, UNIT_TILES], F32)
        bias = sb("bias", [TILE, 8], F32)
        bias_out = sb("bias_out", [1, 1], F32)
        listed = sb("listed", [TILE, PAIRS, CHAINS, ACTIVE], I32)
        equal = sb("equal", [TILE, CHAINS, ACTIVE, ACTIVE - 1], F16)
        repeated = sb("repeated", [TILE, CHAINS, ACTIVE], F16)
        rows_wanted = sb("rows_wanted", [TILE, CHAINS, ACTIVE], I32)
        sums = [sb(f"sums{chain}", [TILE, HIDDEN], F32) for chain in range(CHAINS)]
        unit_matrix32 = sb("unit_matrix32", [TILE, TILE], F32)

        hidden_words = hidden_region[:, :, :].rearrange("p k n -> p (k n)")
        stages = [hidden_words[:, hidden_words.shape[1] - PADDED:]]
        stages += [multihot_region[:, HIGHS * COUNTED + 2 * PADDED * i:HIGHS * COUNTED + 2 * PADDED * (i + 1)]
                   .bitcast(F32) for i in range(2)]
        stages += [mlp_region[:, 0:PADDED]]
        w1_sb = mlp_region[:, 0:8 * H1].rearrange("p (k n) -> p k n", n=H1)
        w2_sb = mlp_region[:, 8 * H1:8 * H1 + 4 * H2].rearrange("p (k n) -> p k n", n=H2)
        w3_sb = mlp_region[:, 8 * H1 + 4 * H2:].rearrange("p (k n) -> p k n", n=H3)
        index = hidden_words[0:PAIRS_OF_INDICES, 0:ALL_QUADS].bitcast(I32)
        high_int = hidden_words[0:PAIRS_OF_INDICES, ALL_QUADS:ALL_QUADS + INDEX_PART].bitcast(I32)
        identity_at = hidden_words.shape[1] - PADDED - TILE // 2
        identity = hidden_words[:, identity_at:identity_at + TILE // 2].bitcast(F16)
        assert ALL_QUADS + INDEX_PART <= identity_at and identity_at + TILE // 2 <= H1 // TILE * CHUNK
        split = small_region[:, :].rearrange("p (s h n) -> p s h n", s=2, h=2)
        hidden2 = small_region[:, 0:2 * 2 * CHUNK].bitcast(F32).rearrange("p (k n) -> p k n", n=CHUNK)
        hidden3 = small_region[:, 4 * CHUNK:6 * CHUNK].bitcast(F32)
        scores = hidden2[0:1, 0, :]

        transform_banks = pb("transform", [TILE, 2, CHUNK], F32)
        transform = transform_banks[:, :, 0:COUNTED]
        counts = pb("counts", [TILE, 2, GROUP, COUNT_STRIDE], F32)
        layer = pb("layer", [TILE, 2, CHUNK], F32)
        turned = [layer[:, i, :].bitcast(F16)[:, 0:SECTION_COLUMNS] for i in range(2)]

        index_loaded = sem("index_loaded")
        codes_loaded = sem("codes_loaded")
        identity_loaded = sem("identity_loaded")
        first_stage_loaded = [sem(f"first_stage{s}_loaded") for s in range(SECTIONS)]
        stage_loaded = [None] + [sem(f"stage{m}_loaded") for m in range(1, UNIT_TILES)]
        mlp_loaded = sem("mlp_loaded")
        bias_loaded = sem("bias_loaded")
        pad_cleared = sem("pad_cleared")
        index_steps = sem("index_steps")
        onehots_ready = sem("onehots_ready")
        counted = sem("counted")
        multihot_ready = sem("multihot_ready")
        maxima_found = sem("maxima_found")
        scale_steps = sem("scale_steps")
        listed_loaded = sem("listed_loaded")
        equal_cleared = sem("equal_cleared")
        repeat_steps = sem("repeat_steps")
        rows_ready = sem("rows_ready")
        gathered = [sem(f"gathered{chain}") for chain in range(CHAINS)]
        sums_turned = sem("sums_turned")
        sums_clipped = sem("sums_clipped")
        high_split = sem("high_split")
        low_split = sem("low_split")
        pool_split = sem("pool_split")
        section_scaled = sem("section_scaled")
        high_turned = sem("high_turned")
        low_turned = sem("low_turned")
        high_placed = sem("high_placed")
        low_placed = sem("low_placed")
        transform_done = sem("transform_done")
        transform_read = sem("transform_read")
        hidden0_ready = sem("hidden0_ready")
        layer_done = sem("layer_done")
        layer_read = sem("layer_read")
        stored = sem("stored")

        LAYER_BANKS = H1 // TILE + H2 // TILE + H3 // TILE + 1

        def wait_low_split(engine, n):
            if vector_splits(n) > 0:
                engine.wait_ge(low_split, vector_splits(n))
            if n in POOL_SECTIONS:
                engine.wait_ge(pool_split, POOL_SECTIONS.index(n) + 1)

        block = ctx.enter_context(nc.Block())

        @block.sync
        def _(sp):
            sp.dma_start(index, indices).then_inc(index_loaded, 16)
            for s in range(SECTIONS):
                columns = slice(s * SECTION_COLUMNS, min((s + 1) * SECTION_COLUMNS, FEATURES))
                sp.dma_start(stages[0][:, columns], ft_w[0:TILE, columns]).then_inc(first_stage_loaded[s], 16)
            sp.dma_start(listed[:, :, :, :], gather_indices).then_inc(listed_loaded, 16)
            for m in range(1, UNIT_TILES):
                sp.dma_start(stages[m][:, 0:FEATURES], ft_w[m * TILE:(m + 1) * TILE, :])\
                    .then_inc(stage_loaded[m], 16)
            sp.wait_ge(high_split, UNIT_TILES * SECTIONS)
            wait_low_split(sp, UNIT_TILES * SECTIONS - 1)
            sp.dma_start(w1_sb, w1).then_inc(mlp_loaded, 16)
            sp.dma_start(w2_sb, w2).then_inc(mlp_loaded, 16)
            sp.dma_start(w3_sb, w3).then_inc(mlp_loaded, 16)

            with sp.Fori(0, PAIRS) as pair:
                sp.wait_ge(layer_read, LAYER_BANKS * pair + LAYER_BANKS)
                sp.dma_start(out[0:1, bass.ds(pair * CHUNK, CHUNK)], scores).then_inc(stored, 16)
            sp.wait_ge(stored, 16 * PAIRS)

        @block.gpsimd
        def _(pool):
            for stage in stages:
                nc.gpsimd.memset(stage[:, FEATURES:PADDED], 0.0).then_inc(pad_cleared, 1)
            nc.gpsimd.memset(equal[:, :, :, :], 0.0).then_inc(equal_cleared, 1)
            nc.gpsimd.memset(unit_matrix32[:, :], 0.0).then_inc(equal_cleared, 1)
            pool.wait_ge(equal_cleared, 2)
            nc.gpsimd.affine_select(out=unit_matrix32[:, :], in_=unit_matrix32[:, :], compare_op=ALU.not_equal,
                                    fill=1.0, base=0, pattern=[[-1, TILE]], channel_multiplier=1)\
                .then_inc(equal_cleared, 1)

            for i, n in enumerate(POOL_SECTIONS):
                m, s = divmod(n, SECTIONS)
                section = stages[m][:, s * SECTION_COLUMNS:(s + 1) * SECTION_COLUMNS]
                pool.wait_ge(high_split, n + 1)
                nc.gpsimd.tensor_scalar(section, section, scale[:, m:m + 1], 1.0, ALU.mult, ALU.mult)\
                    .then_inc(section_scaled, 1)
                pool.wait_ge(section_scaled, i + 1)
                if n >= 2:
                    pool.wait_ge(low_turned, n - 1)
                nc.gpsimd.tensor_tensor(split[:, n % 2, 1, :], section, split[:, n % 2, 0, :],
                                        ALU.subtract).then_inc(pool_split, 1)

            with pool.Fori(0, PAIRS) as pair:
                pool.wait_ge(rows_ready, pair + 1)
                for j in range(ACTIVE):
                    for chain in range(CHAINS):
                        if j:
                            pool.wait_ge(gathered[chain], 16 * ACTIVE * pair + 16 * j)
                        pool.nop(nofuse=True)
                        nc.gpsimd.indirect_dma_start(
                            out=sums[chain][:, :], out_offset=None, in_=feature_rows,
                            in_offset=bass.IndirectOffsetOnAxis(ap=rows_wanted[:, chain, j:j + 1], axis=0),
                            compute_op=ALU.add if j else ALU.bypass).then_inc(gathered[chain], 16)

        @block.vector
        def _(dve):
            def split_indices(part, first, size):
                quads = slice(first, first + size)
                to = slice(0, size)
                nc.vector.tensor_scalar(high_int[:, to], index[:, quads], 7, None,
                                        ALU.arith_shift_right).then_inc(index_steps, 1)
                dve.wait_ge(index_steps, 3 * part + 1)
                nc.vector.tensor_copy(high[:, quads], high_int[:, to]).then_inc(index_steps, 1)
                dve.wait_ge(index_steps, 3 * part + 2)
                nc.vector.scalar_tensor_tensor(out=low[:, quads], in0=high[:, quads], scalar=-float(TILE),
                                               in1=index[:, quads], op0=ALU.mult, op1=ALU.add)\
                    .then_inc(index_steps, 1)
                dve.wait_ge(index_steps, 3 * part + 3)

            def compare(group, slot, ring_full=True):
                if ring_full:
                    dve.wait_ge(counted, group - (RING - 1))
                quads = bass.ds(group * GROUP, GROUP)
                nc.vector.tensor_tensor(
                    high_hot[:, slot, :, :], high_codes,
                    high[:, quads].unsqueeze(1).to_broadcast([PAIRS_OF_INDICES, COUNTS, GROUP]), ALU.is_equal)
                nc.vector.tensor_tensor(
                    low_hot[:, slot, :, :], low_codes,
                    low[:, quads].unsqueeze(1).to_broadcast([PAIRS_OF_INDICES, TILE, GROUP]), ALU.is_equal)\
                    .then_inc(onehots_ready, 1)

            def section_maximum(m, s):
                if m == 0:
                    dve.wait_ge(first_stage_loaded[s], 16)
                else:
                    dve.wait_ge(stage_loaded[m], 16)
                dve.wait_ge(pad_cleared, m + 1)
                nc.vector.tensor_reduce(section_largest[:, m, s:s + 1],
                                        stages[m][:, s * SECTION_COLUMNS:(s + 1) * SECTION_COLUMNS], AX.X,
                                        ALU.max, apply_absolute_value=True).then_inc(maxima_found, 1)

            def weight_scale(m):
                dve.wait_ge(maxima_found, SECTIONS * (m + 1))
                column = slice(m, m + 1)
                nc.vector.tensor_reduce(largest[:, column], section_largest[:, m, :], AX.X, ALU.max)\
                    .then_inc(scale_steps, 1)
                dve.wait_ge(scale_steps, 4 * m + 1)
                nc.vector.tensor_scalar(power[:, column], largest[:, column].bitcast(I32), 0xFF << 23, None,
                                        ALU.bitwise_and).then_inc(scale_steps, 1)
                dve.wait_ge(scale_steps, 4 * m + 2)
                nc.vector.tensor_scalar(unscale[:, column].bitcast(I32), power[:, column],
                                        float((SCALED_EXPONENT + 1) << 23), float(SCALED_EXPONENT << 23),
                                        ALU.max, ALU.subtract).then_inc(scale_steps, 1)
                dve.wait_ge(scale_steps, 4 * m + 3)
                nc.vector.tensor_scalar(scale[:, column].bitcast(I32), unscale[:, column].bitcast(I32),
                                        -1.0, float(MAX_FLOAT_EXPONENT_PAIR << 23),
                                        ALU.mult, ALU.add).then_inc(scale_steps, 1)
                dve.wait_ge(scale_steps, 4 * m + 4)

            def split_low(n):
                if n in POOL_SECTIONS:
                    return
                m, s = divmod(n, SECTIONS)
                dve.wait_ge(high_split, n + 1)
                if n >= 2:
                    dve.wait_ge(low_turned, n - 1)
                nc.vector.scalar_tensor_tensor(
                    out=split[:, n % 2, 1, :], in0=stages[m][:, s * SECTION_COLUMNS:(s + 1) * SECTION_COLUMNS],
                    scalar=scale[:, m:m + 1], in1=split[:, n % 2, 0, :],
                    op0=ALU.mult, op1=ALU.subtract).then_inc(low_split, 1)

            def find_rows(pair):
                for d in range(1, ACTIVE):
                    last = nc.vector.tensor_tensor(
                        equal[:, :, d:ACTIVE, d - 1], listed[:, bass.ds(pair, 1), :, d:ACTIVE].squeeze(1),
                        listed[:, bass.ds(pair, 1), :, 0:ACTIVE - d].squeeze(1), ALU.is_equal)
                last.then_inc(repeat_steps, 1)
                dve.wait_ge(repeat_steps, 2 * pair + 1)
                nc.vector.tensor_reduce(repeated[:, :, :], equal[:, :, :, :], AX.X, ALU.max)\
                    .then_inc(repeat_steps, 1)
                dve.wait_ge(repeat_steps, 2 * pair + 2)
                nc.vector.scalar_tensor_tensor(
                    out=rows_wanted[:, :, :], in0=repeated[:, :, :], scalar=float(FEATURES),
                    in1=listed[:, bass.ds(pair, 1), :, :].squeeze(1), op0=ALU.mult, op1=ALU.max)\
                    .then_inc(rows_ready, 1)

            def clip_sums(pair):
                for chain in range(CHAINS):
                    dve.wait_ge(sums_turned, CHAINS * pair + chain + 1)
                    if chain < SIDES:
                        to = hidden0[:, UNIT_TILES * chain:UNIT_TILES * (chain + 1), COUNTED:COUNTED + TILE]
                        units = layer[:, chain, :].rearrange("p (m n) -> p m n", n=TILE)
                    else:
                        to = hidden0[:, :, COUNTED + TILE:CHUNK].rearrange("p (s m) n -> p s m n", s=SIDES)
                        units = layer[:, 0, :].rearrange("p (m s n) -> p s m n", s=SIDES, m=UNIT_TILES)
                    nc.vector.tensor_scalar(to, units, 1.0, -1.0, ALU.min, ALU.max).then_inc(sums_clipped, 1)

            def clip(unit_tile, bank, row, m):
                dve.wait_ge(transform_done, unit_tile + 1)
                nc.vector.tensor_scalar(hidden0[:, row, 0:COUNTED], transform[:, bank, :],
                                        unscale[:, bass.ds(m, 1)], 1.0, ALU.mult, ALU.min)\
                    .then_inc(transform_read, 1)
                dve.wait_ge(transform_read, unit_tile + 1)
                nc.vector.tensor_scalar(hidden0[:, row, 0:COUNTED], hidden0[:, row, 0:COUNTED], -1.0, None, ALU.max)\
                    .then_inc(hidden0_ready, 1)

            dve.wait_ge(index_loaded, 16)
            split_indices(0, 0, QUADS)
            dve.wait_ge(codes_loaded, 16)
            for g in range(EARLY_GROUPS):
                compare(g, g % RING, g >= RING)
                for section in EARLY_MAXIMA.get(g, ()):
                    section_maximum(0, section)
                if g == SCALE_AFTER:
                    weight_scale(0)
            split_low(0)
            for s in range(SECTIONS):
                if s == FIRST_ROWS_AT:
                    dve.wait_ge(listed_loaded, 16)
                    dve.wait_ge(equal_cleared, 1)
                    find_rows(0)
                if s + 1 < SECTIONS:
                    split_low(s + 1)
                for g in second_groups(s):
                    compare(g, g % RING)
            for s in range(SECTIONS):
                for g in third_groups(s):
                    compare(g, g % RING)
                section_maximum(1, s)
            weight_scale(1)
            split_low(SECTIONS)
            for g in first_chunk_groups(0):
                compare(GROUPS + g, g % RING)
            for n in range(UNIT_TILES * SECTIONS):
                m, s = divmod(n, SECTIONS)
                for t in turned_after(n):
                    if t + 1 < UNIT_TILES * SECTIONS:
                        split_low(t + 1)
                if n + 1 < UNIT_TILES * SECTIONS:
                    for g in first_chunk_groups(n + 1):
                        compare(GROUPS + g, g % RING)
                for section in LATER_MAXIMA.get(n, ()):
                    section_maximum(*section)
                    if section[1] == SECTIONS - 1:
                        weight_scale(section[0])
                if n == SECTIONS - 1:
                    split_indices(1, QUADS, INDEX_PART)
                    split_indices(2, QUADS + INDEX_PART, INDEX_PART)
                if s == SECTIONS - 1:
                    clip(m, m % 2, m, m)

            def products_of(chunk, side, half, parity, before_clip=None):
                m = 2 * half + parity
                for j in range(TILE_GROUPS * parity, TILE_GROUPS * (parity + 1)):
                    compare(GROUPS * chunk + GROUPS + 2 * TILE_GROUPS * half + j, j % RING)
                if before_clip is not None:
                    clip_sums(before_clip)
                clip(UNIT_TILES * chunk + m, parity, UNIT_TILES * side + m, m)

            with dve.Fori(0, PAIRS - 1) as pair:
                for m in range(UNIT_TILES):
                    products_of(2 * pair + 1, 1, m // 2, m % 2, pair if m == UNIT_TILES - 1 else None)
                find_rows(pair + 1)
                with dve.Fori(0, UNIT_TILES // 2) as half:
                    for parity in range(2):
                        products_of(2 * pair + 2, 0, half, parity)
            for m in range(UNIT_TILES):
                if m == UNIT_TILES - 1:
                    clip_sums(PAIRS - 1)
                clip(UNIT_TILES * (2 * PAIRS - 1) + m, m % 2, UNIT_TILES + m, m)

        @block.scalar
        def _(act):
            act.dma_start(codes[:, :, :], code_table).then_inc(codes_loaded, 16)
            act.dma_start(identity, unit_matrix).then_inc(identity_loaded, 16)
            act.dma_start(bias[:, :], biases).then_inc(bias_loaded, 16)
            act.dma_start(bias_out[:, :], bo).then_inc(bias_loaded, 16)

            def place_multihot(group, bank, quad_columns, side):
                act.wait_ge(counted, group + 1)
                nc.scalar.activation(
                    multihot[side][:, :, quad_columns].rearrange("p h (q b) -> p h q b", b=ROWS),
                    counts[:, bank, :, 0:COUNTS].rearrange("p q (h b) -> p h q b", b=ROWS),
                    ACT.Sign).then_inc(multihot_ready, 1)

            def split_high(n):
                m, s = divmod(n, SECTIONS)
                if s == 0:
                    act.wait_ge(scale_steps, 4 * m + 4)
                if n >= 2:
                    wait_low_split(act, n - 2)
                    act.wait_ge(high_turned, n - 1)
                columns = slice(s * SECTION_COLUMNS, (s + 1) * SECTION_COLUMNS)
                nc.scalar.activation(split[:, n % 2, 0, :], stages[m][:, columns], ACT.Copy,
                                     scale=scale[:, m:m + 1]).then_inc(high_split, 1)

            def place(n, part, was_turned, was_placed):
                m, s = divmod(n, SECTIONS)
                act.wait_ge(was_turned, n + 1)
                nc.scalar.activation(weights[:, part, s * SECTION:(s + 1) * SECTION, m * TILE:(m + 1) * TILE],
                                     turned[part].rearrange("p (k n) -> p k n", n=TILE), ACT.Copy)\
                    .then_inc(was_placed, 1)

            def columns_of(g):
                return slice(g * GROUP * ROWS, (g + 1) * GROUP * ROWS)

            def columns_at(g):
                return bass.ds(g * (GROUP * ROWS), GROUP * ROWS)

            for g in range(EARLY_GROUPS):
                place_multihot(g, g % 2, columns_of(g), 0)
            split_high(0)
            split_high(1)
            for s in range(SECTIONS):
                place(s, 0, high_turned, high_placed)
                if s + 2 < SECTIONS:
                    split_high(s + 2)
                place(s, 1, low_turned, low_placed)
                for g in second_groups(s):
                    place_multihot(g, g % 2, columns_of(g), 0)
            for s in range(SECTIONS):
                for g in third_groups(s):
                    place_multihot(g, g % 2, columns_of(g), 0)
            split_high(SECTIONS)
            split_high(SECTIONS + 1)
            for n in range(UNIT_TILES * SECTIONS):
                groups = first_chunk_groups(n)
                if groups and groups[0] == 0:
                    wait_low_split(act, 3 * SECTIONS - 1)
                for g in groups:
                    place_multihot(GROUPS + g, g % 2, columns_of(g), 1)
                for t in turned_after(n):
                    place(t, 0, high_turned, high_placed)
                    if t + 2 < UNIT_TILES * SECTIONS:
                        split_high(t + 2)
                    place(t, 1, low_turned, low_placed)

            def place_groups(first_group, side):
                with act.Fori(0, UNIT_TILES // 2) as half:
                    for j in range(2 * TILE_GROUPS):
                        g = 2 * TILE_GROUPS * half + j
                        place_multihot(first_group + g, j % 2, columns_at(g), side)

            def relu_bank(pair, bank_number, to):
                act.wait_ge(layer_done, LAYER_BANKS * pair + bank_number + 1)
                nc.scalar.activation(to, layer[:, bank_number % 2, :], ACT.Relu,
                                     bias=bias[:, bank_number:bank_number + 1]).then_inc(layer_read, 1)

            def relu_layers(pair):
                for t in range(H1 // TILE):
                    relu_bank(pair, t, hidden1[:, t, :])
                for t in range(H2 // TILE):
                    relu_bank(pair, 4 + t, hidden2[:, t, :])
                relu_bank(pair, 6, hidden3)

            def score(pair):
                act.wait_ge(layer_done, LAYER_BANKS * pair + LAYER_BANKS)
                nc.scalar.activation(scores, layer[0:1, 1, :], ACT.Identity, bias=bias_out[:, :])\
                    .then_inc(layer_read, 1)

            act.wait_ge(bias_loaded, 32)
            with act.Fori(0, PAIRS - 1) as pair:
                place_groups(GROUPS * (2 * pair + 2), 0)
                relu_layers(pair)
                place_groups(GROUPS * (2 * pair + 3), 1)
                score(pair)
                act.wait_ge(stored, 16 * pair + 16)
            relu_layers(PAIRS - 1)
            score(PAIRS - 1)

        @block.tensor
        def _(pe):
            def count(group, slot, bank, first=False):
                pe.wait_ge(onehots_ready, group + 1)
                if not first:
                    pe.wait_ge(multihot_ready, group - 1)
                for q in range(GROUP):
                    last = nc.tensor.matmul(counts[:, bank, q, 0:COUNTS], low_hot[:, slot, :, q],
                                            high_hot[:, slot, :, q], start=True, stop=True)
                last.then_inc(counted, 1)

            def turn(n):
                for part, was_placed, was_turned in ((0, high_placed, high_turned), (1, low_placed, low_turned)):
                    if part == 0:
                        pe.wait_ge(high_split, n + 1)
                    else:
                        wait_low_split(pe, n)
                    if n:
                        pe.wait_ge(was_placed, n)
                    for k in range(SECTION):
                        last = nc.tensor.transpose(turned[part][:, k * TILE:(k + 1) * TILE],
                                                   split[:, n % 2, part, k * TILE:(k + 1) * TILE],
                                                   identity)
                    last.then_inc(was_turned, 1)

            def multiply(side, units, bank, s, positions=slice(0, COUNTED), between=()):
                between = list(between)
                for k in range(s * SECTION, (s + 1) * SECTION):
                    for part in range(2):
                        last = nc.tensor.matmul(transform[:, bank, positions], weights[:, part, k, units],
                                                multihot[side][:, k, positions],
                                                start=(k == 0 and part == 0),
                                                stop=(k == HIGHS - 1 and part == 1))
                    if between and (k - s * SECTION) % 2 == 1:
                        count(*between.pop(0))
                for group in between:
                    count(*group)
                return last

            for g in range(EARLY_GROUPS):
                count(g, g % RING, g % 2, first=g < 2)
            pe.wait_ge(identity_loaded, 16)
            first_half = slice(0, COUNTED // 2)
            second_half = slice(COUNTED // 2, COUNTED)

            def multiply_first_half(s):
                if s == 0:
                    pe.wait_ge(multihot_ready, GROUPS // 2)
                pe.wait_ge(high_placed, s + 1)
                pe.wait_ge(low_placed, s + 1)
                multiply(0, slice(0, TILE), 0, s, first_half, [(g, g % RING, g % 2) for g in third_groups(s)])

            for s in range(SECTIONS):
                turn(s)
                for g in second_groups(s):
                    count(g, g % RING, g % 2)
                if s >= SECTIONS - HALF_FROM:
                    multiply_first_half(s - (SECTIONS - HALF_FROM))
            for s in range(HALF_FROM, SECTIONS):
                multiply_first_half(s)
            pe.wait_ge(multihot_ready, GROUPS)
            for n in range(UNIT_TILES * SECTIONS):
                m, s = divmod(n, SECTIONS)
                if m >= 2 and s == 0:
                    pe.wait_ge(transform_read, m - 1)
                if m > 0:
                    pe.wait_ge(high_placed, n + 1)
                    pe.wait_ge(low_placed, n + 1)
                last = multiply(0, slice(m * TILE, (m + 1) * TILE), m % 2, s,
                                slice(0, COUNTED) if m > 0 else second_half,
                                [(GROUPS + g, g % RING, g % 2) for g in first_chunk_groups(n)])
                if s == SECTIONS - 1:
                    last.then_inc(transform_done, 1)
                for t in turned_after(n):
                    turn(t)

            def multiply_unit_tile(chunk, side, half, parity, sums_of=None):
                m = 2 * half + parity
                pe.wait_ge(transform_read, UNIT_TILES * chunk + m - 1)
                counts_made = 0
                for s in range(SECTIONS):
                    if sums_of is not None:
                        turn_sums(sums_of, SUMS_BEFORE[s])
                    last = multiply(side, bass.ds(m * TILE, TILE), parity, s)
                    if s == SECTIONS - 1:
                        last.then_inc(transform_done, 1)
                    while counts_made < TILE_GROUPS * (s + 1) // SECTIONS:
                        j = TILE_GROUPS * parity + counts_made
                        count(GROUPS * chunk + GROUPS + 2 * TILE_GROUPS * half + j, j % RING, j % 2)
                        counts_made += 1

            def turn_sums(pair, chains):
                for chain in chains:
                    pe.wait_ge(gathered[chain], 16 * ACTIVE * pair + 16 * ACTIVE)
                    if chain == 2:
                        pe.wait_ge(sums_clipped, CHAINS * pair + 1)
                    for m in range(UNIT_TILES):
                        last = nc.tensor.transpose(layer[:, chain % 2, m * TILE:(m + 1) * TILE],
                                                   sums[chain][:, m * TILE:(m + 1) * TILE], unit_matrix32[:, :])
                    last.then_inc(sums_turned, 1)

            def dense(pair, bank_number, weight, activation, inputs_ready, before):
                tiles = len(weight)
                pe.wait_ge(inputs_ready, before)
                for k in range(tiles):
                    if k == tiles - 1:
                        pe.wait_ge(inputs_ready, before + 1)
                    last = nc.tensor.matmul(layer[:, bank_number % 2, :], weight[k], activation[:, k, :],
                                            start=(k == 0), stop=(k == tiles - 1))
                last.then_inc(layer_done, 1)

            def later_layers(pair):
                banks = LAYER_BANKS * pair
                pe.wait_ge(sums_clipped, CHAINS * pair + CHAINS)
                for t in range(H1 // TILE):
                    if t >= 2:
                        pe.wait_ge(layer_read, banks + t - 1)
                    dense(pair, t, [w1_sb[:, k, t * TILE:(t + 1) * TILE] for k in range(SIDES * UNIT_TILES)],
                          hidden0, hidden0_ready, SIDES * UNIT_TILES * pair + 7)
                for t in range(H2 // TILE):
                    if t == 1:
                        pe.wait_ge(layer_read, banks + 4)
                    dense(pair, 4 + t, [w2_sb[:, k, t * TILE:(t + 1) * TILE] for k in range(H1 // TILE)],
                          hidden1, layer_read, banks + 3)
                dense(pair, 6, [w3_sb[:, k, :] for k in range(H2 // TILE)], hidden2, layer_read, banks + 5)

            def output_layer(pair):
                pe.wait_ge(layer_read, LAYER_BANKS * pair + 7)
                nc.tensor.matmul(layer[0:1, 1, :], bias[:, 7:8], hidden3, start=True, stop=True)\
                    .then_inc(layer_done, 1)

            pe.wait_ge(mlp_loaded, 48)
            pe.wait_ge(equal_cleared, 3)
            pe.wait_ge(bias_loaded, 32)
            with pe.Fori(0, PAIRS - 1) as pair:
                pe.wait_ge(multihot_ready, SIDES * GROUPS * pair + SIDES * GROUPS)
                for m in range(UNIT_TILES):
                    multiply_unit_tile(2 * pair + 1, 1, m // 2, m % 2, pair if m == UNIT_TILES - 1 else None)
                later_layers(pair)
                with pe.Fori(0, UNIT_TILES // 2) as half:
                    pe.wait_ge(multihot_ready, SIDES * GROUPS * pair + (SIDES + 1) * GROUPS)
                    for parity in range(2):
                        multiply_unit_tile(2 * pair + 2, 0, half, parity)
                output_layer(pair)
            pe.wait_ge(layer_read, LAYER_BANKS * (PAIRS - 1))
            pe.wait_ge(multihot_ready, GROUPS * SIDES * PAIRS)
            for m in range(UNIT_TILES):
                pe.wait_ge(transform_read, UNIT_TILES * (SIDES * PAIRS - 1) + m - 1)
                for s in range(SECTIONS):
                    if m == UNIT_TILES - 1:
                        turn_sums(PAIRS - 1, SUMS_BEFORE[s])
                    last = multiply(1, slice(m * TILE, (m + 1) * TILE), m % 2, s)
                last.then_inc(transform_done, 1)
            later_layers(PAIRS - 1)
            output_layer(PAIRS - 1)


TILE_GROUPS = GROUPS // UNIT_TILES
assert 2 * TILE_GROUPS % RING == 0
SUMS_BEFORE = ((), (), (), (0, 1), (2,))
EARLY_GROUPS = 8
LATE_GROUPS = EARLY_GROUPS + 2 * SECTIONS
POOL_SECTIONS = (0, 2, 4)


def vector_splits(n):
    return n + 1 - sum(p <= n for p in POOL_SECTIONS)


EARLY_MAXIMA = {3: (0, 1), 4: (2,), 5: (3, 4)}
LATER_MAXIMA = {n: ((2 + n // SECTIONS, n % SECTIONS),) for n in range(2 * SECTIONS)}
FIRST_ROWS_AT = 2
SCALE_AFTER = 7


def second_groups(s):
    return range(EARLY_GROUPS + 2 * s, EARLY_GROUPS + 2 * s + 2)


def third_groups(s):
    if s < HALF_FROM:
        return range(0)
    rest, steps, s = GROUPS - LATE_GROUPS, SECTIONS - HALF_FROM, s - HALF_FROM
    return range(LATE_GROUPS + rest * s // steps, LATE_GROUPS + rest * (s + 1) // steps)


HALF_FROM = 3


def turned_after(n):
    def through(n):
        return max(SECTIONS, min(UNIT_TILES * SECTIONS, n + 3 + (n >= 7) + (n >= 9)))
    return range(through(n - 1), through(n))


def first_chunk_groups(n):
    first, last = 11, UNIT_TILES * SECTIONS
    if n < first:
        return range(0)
    return range(GROUPS * (n - first) // (last - first), GROUPS * (n - first + 1) // (last - first))


def kernel(**inputs):
    import numpy as np
    import concourse.bacc as bacc
    from concourse.bass_utils import run_bass_kernel_spmd

    def counted(name):
        a = np.asarray(inputs[name]).reshape(PAIRS, CHUNK, ACTIVE)[:, :COUNTED]
        a = a.reshape(PAIRS, QUADS, ROWS, ACTIVE)
        return a.transpose(2, 3, 0, 1).reshape(PAIRS_OF_INDICES, PAIRS, QUADS)

    def gathered(name):
        return np.asarray(inputs[name]).reshape(PAIRS, CHUNK, ACTIVE)[:, COUNTED:].transpose(1, 0, 2)

    white, black = gathered("r_white_indices"), gathered("r_black_indices")
    chains = [white[:TILE], black[:TILE], np.concatenate([white[TILE:], black[TILE:]])]

    def both(side):
        return np.ascontiguousarray(np.stack([side("r_white_indices"), side("r_black_indices")], axis=2))

    def tiled(name):
        a = np.asarray(inputs["L0_rec_" + name]).T
        return np.ascontiguousarray(a.reshape(-1, TILE, a.shape[1]).transpose(1, 0, 2))

    def columns(name):
        return np.asarray(inputs["L0_rec_" + name]).reshape(-1, TILE).T

    owner = np.arange(PAIRS_OF_INDICES)[:, None, None] // ACTIVE
    high_codes = np.where(np.arange(ROWS)[None, None, :] == owner, np.arange(HIGHS)[None, :, None], -1)
    low_codes = np.broadcast_to(np.arange(TILE), (PAIRS_OF_INDICES, TILE))
    codes = np.concatenate([high_codes.reshape(PAIRS_OF_INDICES, COUNTS), low_codes], axis=1)

    arrays = {
        "indices": both(counted).reshape(PAIRS_OF_INDICES, ALL_QUADS),
        "gather_indices": np.ascontiguousarray(np.stack(chains, axis=2)),
        "codes": np.repeat(codes[:, :, None], GROUP, axis=2).astype(np.float16),
        "identity": np.eye(TILE, dtype=np.float16),
        "ft_w": np.ascontiguousarray(inputs["L0_rec_ft_w"]),
        "feature_rows": np.pad(np.asarray(inputs["L0_rec_ft_w"]).T, ((0, 1), (0, 0))),
        "w1": tiled("w1"), "w2": tiled("w2"), "w3": tiled("w3"),
        "biases": np.ascontiguousarray(np.concatenate(
            [columns("b1"), columns("b2"), columns("b3"), columns("wo")], axis=1)),
        "bo": np.asarray(inputs["L0_rec_bo"]).reshape(1, 1),
    }
    nc = bacc.Bacc("TRN2", target_bir_lowering=False, num_devices=1)
    args = {name: nc.dram_tensor(f"{name}_dram", a.shape, mybir.dt.from_np(a.dtype), kind="ExternalInput").ap()
            for name, a in arrays.items()}
    out = nc.dram_tensor("scores_dram", (1, BATCH), mybir.dt.float32, kind="ExternalOutput").ap()
    nnue_kernel(nc, *args.values(), out)
    result = run_bass_kernel_spmd(nc, [{f"{name}_dram": a for name, a in arrays.items()}], core_ids=[0])
    return result.results[0]["scores_dram"].reshape(BATCH)
```
